# Optimizing a Trainium2 kernel written in Bass

```python
import numpy as np
import jax
import jax.numpy as jnp

def _softmax(x, axis=-1):
    return jax.nn.softmax(x, axis=axis)

def _gelu(x):
    return jax.nn.gelu(x, approximate=True)

def _silu(x):
    return jax.nn.silu(x)

def _sigmoid(x):
    return jax.nn.sigmoid(x)

def _layernorm(x, axis=-1, eps=1e-05):
    m = jnp.mean(x, axis=axis, keepdims=True)
    v = jnp.var(x, axis=axis, keepdims=True)
    return (x - m) / jnp.sqrt(v + eps)

def _scatter_add(tgt, idx, src, axis=0):
    return tgt.at[idx].add(src)

def _segment_sum(src, seg, n):
    return jax.ops.segment_sum(src, seg, n)
kernel_name = 'mk_xattn_ffn_d2_seqx_r8_1f17cd'

def setup_inputs(seed: int=0):
    np.random.seed(seed)
    _w = jnp.asarray

    def _rec_inputs():
        import jax
        import jax.numpy as jnp
        _rk = jax.random.key(seed)
        x = -7.109e-05 + 0.9999 * jax.random.normal(jax.random.fold_in(_rk, 1), (8, 128, 512), jnp.float32)
        _lenS = 128 - jax.random.randint(jax.random.fold_in(_rk, 7), (8,), 0, max(1, 128 // 4) + 1, jnp.int32)
        _lenS2 = 128 - jax.random.randint(jax.random.fold_in(_rk, 8), (8,), 0, max(1, 128 // 4) + 1, jnp.int32)
        _ctx_4096P = jax.random.normal(jax.random.fold_in(_rk, 11), (8, 16, 512), jnp.float32)
        _ctx_4096c = jax.random.dirichlet(jax.random.fold_in(_rk, 511), 0.3 * jnp.ones((16,), jnp.float32), (8, 128))
        _ctx_4096t = jnp.einsum('bsk,bkd->bsd', _ctx_4096c, _ctx_4096P)
        _ctx_4096t = _ctx_4096t * jax.lax.rsqrt(jnp.mean(jnp.square(_ctx_4096t)) + 1e-12) * 0.953939
        ctx_4096 = -2.6191e-05 + 0.999952 * (_ctx_4096t + 0.3 * jax.random.normal(jax.random.fold_in(_rk, 611), (8, 128, 512), jnp.float32))
        _validS = jnp.arange(128)[None, :] < _lenS[:, None]
        _validS2 = jnp.arange(128)[None, :] < _lenS2[:, None]
        _causal = jnp.tril(jnp.ones((128, 128), dtype=bool))
        mask_1x1xSxS2_ff0 = jnp.where(jnp.ones((1, 1, 128, 128), dtype=bool), 0.0, -1000000000.0).astype(jnp.float32)
        return (x, ctx_4096, mask_1x1xSxS2_ff0)
    x, ctx_4096, mask_1x1xSxS2_ff0 = _rec_inputs()

    def _L0_xattn_setup():
        import jax, jax.numpy as jnp
        import numpy as np
        TEXT_DIM = 512
        FEATURE_DIM = 512

        def _xavier_uniform(key, shape):
            fan_in, fan_out = (shape[1], shape[0])
            limit = float(np.sqrt(6.0 / (fan_in + fan_out)))
            return jax.random.uniform(key, shape, jnp.float32, -limit, limit)
        key = jax.random.key(seed)
        k1, k2, k3, k4 = jax.random.split(key, 4)
        text = jax.random.normal(k1, (8, 256, TEXT_DIM), jnp.float32)
        features = jax.random.normal(k2, (8, 72, FEATURE_DIM), jnp.float32)
        Wq = _xavier_uniform(k3, (FEATURE_DIM, TEXT_DIM))
        bq = jnp.zeros((FEATURE_DIM,), jnp.float32)
        Wk = _xavier_uniform(k4, (FEATURE_DIM, FEATURE_DIM))
        bk = jnp.zeros((FEATURE_DIM,), jnp.float32)
        return {'text': text, 'features': features, 'Wq': Wq, 'bq': bq, 'Wk': Wk, 'bk': bk}
    _L0_xattn_all = _L0_xattn_setup()
    _L0_xattn_in = {k: v for k, v in _L0_xattn_all.items() if k in ('Wq', 'bq', 'Wk', 'bk')}
    del _L0_xattn_all

    def _L0_ffn_setup():
        import jax, jax.numpy as jnp
        import numpy as np
        RANKS = (8, 16, 32, 64)
        TOPK = 1
        SCALING = 1.0 / 4
        key = jax.random.key(seed)
        ks = jax.random.split(key, 7)
        D_IN, D_OUT, MAX_R, N_RANKS = (512, 512, 64, len(RANKS))
        B_, S_ = (4, 256)
        return {'hidden_states': jax.random.normal(ks[0], (B_, S_, D_IN), jnp.float32), 'W': jax.random.normal(ks[1], (D_OUT, D_IN), jnp.float32) * 0.02, 'b': jax.random.normal(ks[2], (D_OUT,), jnp.float32) * 0.02, 'A': jax.random.normal(ks[3], (MAX_R, D_IN), jnp.float32) * 0.02, 'B': jnp.zeros((D_OUT, MAX_R), jnp.float32) + jax.random.normal(ks[4], (D_OUT, MAX_R), jnp.float32) * 0.02, 'gate_w': jax.random.normal(ks[5], (N_RANKS, D_IN), jnp.float32) * 0.02, 'gate_b': jax.random.normal(ks[6], (N_RANKS,), jnp.float32) * 0.02}
    _L0_ffn_all = _L0_ffn_setup()
    _L0_ffn_in = {k: v for k, v in _L0_ffn_all.items() if k in ('W', 'b', 'A', 'B', 'gate_w', 'gate_b')}
    del _L0_ffn_all

    def _L1_xattn_setup():
        import jax, jax.numpy as jnp
        import numpy as np
        NUM_HEADS = 32
        NUM_KV_HEADS = 8
        HEAD_DIM = 128
        HIDDEN = 512
        EPS = 1e-05

        def rmsnorm(x, w, eps=EPS):
            xf = x.astype(jnp.float32)
            var = jnp.mean(xf * xf, axis=-1, keepdims=True)
            return w * (xf * jax.lax.rsqrt(var + eps)).astype(x.dtype)
        key = jax.random.key(seed)
        ks = jax.random.split(key, 10)
        B, Q, KV = (1, 128, 6404)
        s = 1.0 / np.sqrt(HIDDEN)
        return {'hidden_states': jax.random.normal(ks[0], (B, Q, HIDDEN), jnp.float32), 'cross_attention_states': jax.random.normal(ks[1], (B, KV, HIDDEN), jnp.float32), 'attention_mask': jnp.zeros((B, 1, Q, KV), jnp.float32), 'q_proj_w': jax.random.normal(ks[2], (NUM_HEADS * HEAD_DIM, HIDDEN), jnp.float32) * s, 'k_proj_w': jax.random.normal(ks[3], (NUM_KV_HEADS * HEAD_DIM, HIDDEN), jnp.float32) * s, 'v_proj_w': jax.random.normal(ks[4], (NUM_KV_HEADS * HEAD_DIM, HIDDEN), jnp.float32) * s, 'o_proj_w': jax.random.normal(ks[5], (HIDDEN, NUM_HEADS * HEAD_DIM), jnp.float32) * s, 'q_norm_w': jnp.ones((HEAD_DIM,), jnp.float32), 'k_norm_w': jnp.ones((HEAD_DIM,), jnp.float32)}
    _L1_xattn_all = _L1_xattn_setup()
    _L1_xattn_in = {k: v for k, v in _L1_xattn_all.items() if k in ('q_proj_w', 'k_proj_w', 'v_proj_w', 'o_proj_w', 'q_norm_w', 'k_norm_w')}
    del _L1_xattn_all

    def _L1_ffn_setup():
        import jax, jax.numpy as jnp
        import numpy as np
        GROUP_SIZE = 128

        def dequantize(imatrix, scales, zeros, group_size, out_dtype):
            rs = jnp.repeat(scales, group_size, axis=0)
            rz = jnp.repeat(zeros, group_size, axis=0)
            return ((imatrix.astype(rs.dtype) - rz.astype(rs.dtype)) * rs).astype(out_dtype)
        key = jax.random.key(seed)
        ks = jax.random.split(key, 10)
        H, I, G = (512, 1792, GROUP_SIZE)
        B, S = (4, 256)
        x = jax.random.normal(ks[0], (B, S, H), dtype=jnp.float32)
        gate_w = jax.random.randint(ks[1], (H, I), 0, 16, dtype=jnp.int32)
        gate_z = jax.random.randint(ks[2], (H // G, I), 0, 16, dtype=jnp.int32)
        gate_s = jax.random.uniform(ks[3], (H // G, I), dtype=jnp.float32) * 0.01
        up_w = jax.random.randint(ks[4], (H, I), 0, 16, dtype=jnp.int32)
        up_z = jax.random.randint(ks[5], (H // G, I), 0, 16, dtype=jnp.int32)
        up_s = jax.random.uniform(ks[6], (H // G, I), dtype=jnp.float32) * 0.01
        down_w = jax.random.randint(ks[7], (I, H), 0, 16, dtype=jnp.int32)
        down_z = jax.random.randint(ks[8], (I // G, H), 0, 16, dtype=jnp.int32)
        down_s = jax.random.uniform(ks[9], (I // G, H), dtype=jnp.float32) * 0.01
        return {'x': x, 'gate_w': gate_w, 'gate_z': gate_z, 'gate_s': gate_s, 'up_w': up_w, 'up_z': up_z, 'up_s': up_s, 'down_w': down_w, 'down_z': down_z, 'down_s': down_s}
    _L1_ffn_all = _L1_ffn_setup()
    _L1_ffn_in = {k: v for k, v in _L1_ffn_all.items() if k in ('gate_w', 'gate_z', 'gate_s', 'up_w', 'up_z', 'up_s', 'down_w', 'down_z', 'down_s')}
    del _L1_ffn_all
    return {'x': x, 'ctx_4096': ctx_4096, 'mask_1x1xSxS2_ff0': mask_1x1xSxS2_ff0, 'L0_xattn_Wq': _L0_xattn_in['Wq'], 'L0_xattn_bq': _L0_xattn_in['bq'], 'L0_xattn_Wk': _L0_xattn_in['Wk'], 'L0_xattn_bk': _L0_xattn_in['bk'], 'L0_ffn_W': _L0_ffn_in['W'], 'L0_ffn_b': _L0_ffn_in['b'], 'L0_ffn_A': _L0_ffn_in['A'], 'L0_ffn_B': _L0_ffn_in['B'], 'L0_ffn_gate_w': _L0_ffn_in['gate_w'], 'L0_ffn_gate_b': _L0_ffn_in['gate_b'], 'L1_xattn_q_proj_w': _L1_xattn_in['q_proj_w'], 'L1_xattn_k_proj_w': _L1_xattn_in['k_proj_w'], 'L1_xattn_v_proj_w': _L1_xattn_in['v_proj_w'], 'L1_xattn_o_proj_w': _L1_xattn_in['o_proj_w'], 'L1_xattn_q_norm_w': _L1_xattn_in['q_norm_w'], 'L1_xattn_k_norm_w': _L1_xattn_in['k_norm_w'], 'L1_ffn_gate_w': _L1_ffn_in['gate_w'], 'L1_ffn_gate_z': _L1_ffn_in['gate_z'], 'L1_ffn_gate_s': _L1_ffn_in['gate_s'], 'L1_ffn_up_w': _L1_ffn_in['up_w'], 'L1_ffn_up_z': _L1_ffn_in['up_z'], 'L1_ffn_up_s': _L1_ffn_in['up_s'], 'L1_ffn_down_w': _L1_ffn_in['down_w'], 'L1_ffn_down_z': _L1_ffn_in['down_z'], 'L1_ffn_down_s': _L1_ffn_in['down_s']}

def reference(x, ctx_4096, mask_1x1xSxS2_ff0, L0_xattn_Wq, L0_xattn_bq, L0_xattn_Wk, L0_xattn_bk, L0_ffn_W, L0_ffn_b, L0_ffn_A, L0_ffn_B, L0_ffn_gate_w, L0_ffn_gate_b, L1_xattn_q_proj_w, L1_xattn_k_proj_w, L1_xattn_v_proj_w, L1_xattn_o_proj_w, L1_xattn_q_norm_w, L1_xattn_k_norm_w, L1_ffn_gate_w, L1_ffn_gate_z, L1_ffn_gate_s, L1_ffn_up_w, L1_ffn_up_z, L1_ffn_up_s, L1_ffn_down_w, L1_ffn_down_z, L1_ffn_down_s):
    import jax
    import jax.numpy as jnp

    def _L0_xattn_ref(text, features, Wq, bq, Wk, bk):
        import jax, jax.numpy as jnp
        import numpy as np
        TEXT_DIM = 512
        FEATURE_DIM = 512

        def _xavier_uniform(key, shape):
            fan_in, fan_out = (shape[1], shape[0])
            limit = float(np.sqrt(6.0 / (fan_in + fan_out)))
            return jax.random.uniform(key, shape, jnp.float32, -limit, limit)
        Q = jnp.einsum('btx,dx->btd', text, Wq) + bq
        K = jnp.einsum('bpx,dx->bpd', features, Wk) + bk
        scale = 1.0 / jnp.sqrt(jnp.asarray(K.shape[-1], K.dtype))
        scores = jnp.einsum('btd,bpd->btp', Q, K) * scale
        attn = jax.nn.softmax(scores, axis=-1)
        attended = jnp.einsum('btp,bpd->btd', attn, features)
        return attended

    def _L0_ffn_ref(hidden_states, W, b, A, B, gate_w, gate_b):
        import jax, jax.numpy as jnp
        import numpy as np
        RANKS = (8, 16, 32, 64)
        TOPK = 1
        SCALING = 1.0 / 4
        bsz, seq, d_in = hidden_states.shape
        out = jnp.einsum('bsd,od->bso', hidden_states, W) + b
        x = hidden_states.reshape(-1, d_in)
        scores = x @ gate_w.T + gate_b
        probs = jax.nn.softmax(scores, axis=-1)
        routing_weights, selected = jax.lax.top_k(probs, TOPK)
        routing_weights = routing_weights / jnp.sum(routing_weights, axis=-1, keepdims=True)
        lora_outputs = jnp.stack([x @ A[:r, :].T @ B[:, :r].T for r in RANKS], axis=1)
        sel = jnp.take_along_axis(lora_outputs, selected[:, :, None], axis=1)
        final = jnp.sum(sel * routing_weights[:, :, None], axis=1)
        return out + final.reshape(bsz, seq, -1)

    def _L1_xattn_ref(hidden_states, cross_attention_states, attention_mask, q_proj_w, k_proj_w, v_proj_w, o_proj_w, q_norm_w, k_norm_w):
        import jax, jax.numpy as jnp
        import numpy as np
        NUM_HEADS = 32
        NUM_KV_HEADS = 8
        HEAD_DIM = 128
        HIDDEN = 512
        EPS = 1e-05

        def rmsnorm(x, w, eps=EPS):
            xf = x.astype(jnp.float32)
            var = jnp.mean(xf * xf, axis=-1, keepdims=True)
            return w * (xf * jax.lax.rsqrt(var + eps)).astype(x.dtype)
        B, Q, _ = hidden_states.shape
        KV = cross_attention_states.shape[1]
        n_rep = NUM_HEADS // NUM_KV_HEADS
        q = (hidden_states @ q_proj_w.T).reshape(B, Q, NUM_HEADS, HEAD_DIM).transpose(0, 2, 1, 3)
        k = (cross_attention_states @ k_proj_w.T).reshape(B, KV, NUM_KV_HEADS, HEAD_DIM).transpose(0, 2, 1, 3)
        v = (cross_attention_states @ v_proj_w.T).reshape(B, KV, NUM_KV_HEADS, HEAD_DIM).transpose(0, 2, 1, 3)
        q = rmsnorm(q, q_norm_w)
        k = jnp.repeat(k, n_rep, axis=1)
        v = jnp.repeat(v, n_rep, axis=1)
        k = rmsnorm(k, k_norm_w)
        scale = 1.0 / np.sqrt(HEAD_DIM)
        scores = jnp.einsum('bhqd,bhkd->bhqk', q, k) * scale + attention_mask
        attn = jax.nn.softmax(scores.astype(jnp.float32), axis=-1).astype(q.dtype)
        out = jnp.einsum('bhqk,bhkd->bhqd', attn, v)
        out = out.transpose(0, 2, 1, 3).reshape(B, Q, NUM_HEADS * HEAD_DIM)
        return out @ o_proj_w.T

    def _L1_ffn_ref(x, gate_w, gate_z, gate_s, up_w, up_z, up_s, down_w, down_z, down_s):
        import jax, jax.numpy as jnp
        import numpy as np
        GROUP_SIZE = 128

        def dequantize(imatrix, scales, zeros, group_size, out_dtype):
            rs = jnp.repeat(scales, group_size, axis=0)
            rz = jnp.repeat(zeros, group_size, axis=0)
            return ((imatrix.astype(rs.dtype) - rz.astype(rs.dtype)) * rs).astype(out_dtype)
        dt = x.dtype
        gate_proj = dequantize(gate_w, gate_s, gate_z, GROUP_SIZE, dt)
        up_proj = dequantize(up_w, up_s, up_z, GROUP_SIZE, dt)
        down_proj = dequantize(down_w, down_s, down_z, GROUP_SIZE, dt)
        gate = jax.nn.silu(jnp.dot(x, gate_proj))
        up = jnp.dot(x, up_proj)
        return jnp.dot(gate * up, down_proj)
    x = x + _L0_xattn_ref(_layernorm(x, axis=-1), ctx_4096, L0_xattn_Wq, L0_xattn_bq, L0_xattn_Wk, L0_xattn_bk)
    x = x + _L0_ffn_ref(_layernorm(x, axis=-1), L0_ffn_W, L0_ffn_b, L0_ffn_A, L0_ffn_B, L0_ffn_gate_w, L0_ffn_gate_b)
    x = x + _L1_xattn_ref(_layernorm(x, axis=-1), ctx_4096, mask_1x1xSxS2_ff0, L1_xattn_q_proj_w, L1_xattn_k_proj_w, L1_xattn_v_proj_w, L1_xattn_o_proj_w, L1_xattn_q_norm_w, L1_xattn_k_norm_w)
    x = x + _L1_ffn_ref(_layernorm(x, axis=-1), L1_ffn_gate_w, L1_ffn_gate_z, L1_ffn_gate_s, L1_ffn_up_w, L1_ffn_up_z, L1_ffn_up_s, L1_ffn_down_w, L1_ffn_down_z, L1_ffn_down_s)
    return x

_drawn_inputs = setup_inputs


def setup_inputs(seed=0):
    import zlib

    import numpy as np

    out = dict(_drawn_inputs(seed))
    spreads = {'L0_xattn_bq': (0.0, 0.581),
     'L0_xattn_bk': (0.0, 0.8),
     'L1_xattn_q_norm_w': (1.0, 0.2),
     'L1_xattn_k_norm_w': (1.0, 0.2)}
    factors = {'L0_ffn_b': 4.759, 'L0_ffn_gate_w': 3.141, 'L0_ffn_gate_b': 8.0}
    for name, (base, spread) in spreads.items():
        noise = np.random.default_rng([zlib.crc32(name.encode()), seed]).standard_normal(out[name].shape)
        drawn = base * np.exp(spread * noise) if base else spread * noise
        out[name] = jnp.asarray(drawn.astype(out[name].dtype))
    for name, factor in factors.items():
        out[name] = (out[name] * factor).astype(out[name].dtype)
    return out
```

```python
from contextlib import ExitStack

import concourse.bass as bass
from concourse import mybir

F32 = mybir.dt.float32
F32R = mybir.dt.float32r
I32 = mybir.dt.int32
ALU = mybir.AluOpType
ACT = mybir.ActivationFunctionType
AX_X = mybir.AxisListType.X

P = 128
T = 8
HALF = T // 2
D = 512
KT = D // P
TOK = T * P
NKV = 8
REP = 4
RANKS = (8, 16, 32, 64)
RMAX = RANKS[-1]
NR = len(RANKS)
F = 1792
UNITS = F // P
EPS = 1e-5
SCALE0 = 1.0 / float(D) ** 0.5
SCALE1 = 1.0 / float(P) ** 0.5

RING = 4
CTX, WK0, WQ0, WKEY, WFFN, WVAL = 0, 8, 12, 16, 24, 28
WGRP = 36
STEPS = NKV * T
DOWN0 = T + STEPS
BODY = 2 * T


def cross_attention_ffn(nc, x, ctx, ctxT, wk0, wq0, bqk, wkey, wffn, wval, agT, bTb, gate_b, norm_w, mask,
                        wqo, ffn_w, ffn_z, ffn_s, out):
    with ExitStack() as stack:
        def sb(name, shape, dt=F32):
            return stack.enter_context(nc.sbuf_tensor(name, shape, dt))

        def sem(name):
            return stack.enter_context(nc.semaphore(name))

        resid = sb("resid", [P, T, D])
        xnT_hi = sb("xnT_hi", [P, KT, TOK], F32R)
        xnT_lo = sb("xnT_lo", [P, KT, TOK], F32R)
        split = sb("split", [P, 4, 2 * KT * D], F32R)
        kv = sb("kv", [P, 2 * T * KT * 2 * P])
        raw = sb("raw", [P, RING, D])
        sq = sb("sq", [P, D])
        norm = sb("norm", [P, 2, D])
        headT = sb("headT", [P, D])
        score = sb("score", [P, D])
        prob = sb("prob", [P, D])
        probT = sb("probT", [P, D])
        aoT_hi = sb("aoT_hi", [P, D], F32R)
        aoT_lo = sb("aoT_lo", [P, D], F32R)
        vcur = sb("vcur", [P, P])
        ident = sb("ident", [P, P])
        mask_sb = sb("mask_sb", [P, P])
        mhalf = sb("mhalf", [P, T])
        eps = sb("eps", [P, T])
        bias = sb("bias", [P, 2 * KT])
        nw = sb("nw", [P, 2])
        wqk = sb("wqk", [P, 1])
        gb = sb("gb", [P, NR])
        st = sb("st", [P, T, 6])
        mv = sb("mv", [P, T, 2])
        veps = sb("veps", [P, T])
        rstd = sb("rstd", [P, T])
        ssq = sb("ssq", [P, 2, REP])
        msq = sb("msq", [P, 2, REP])
        rms = sb("rms", [P, 2, REP])
        nmax = sb("nmax", [P, T])
        rsum = sb("rsum", [P, T])
        rinv = sb("rinv", [P, T])
        sc = sb("sc", [P, T, NR])
        pmax = sb("pmax", [P, T, NR])
        ind = sb("ind", [P, T, NR - 1])

        QUART = KT * TOK
        q0T = kv[:, 0:QUART].rearrange("p (m n) -> p m n", m=KT)
        k0T = kv[:, QUART:2 * QUART].rearrange("p (m n) -> p m n", m=KT)
        ctxn = kv[:, 2 * QUART:3 * QUART].rearrange("p (b n) -> p b n", b=T)
        xnT32 = kv[:, 3 * QUART:4 * QUART].rearrange("p (m n) -> p m n", m=KT)
        o = 2 * QUART
        hs = kv[:, o:o + T * RMAX].rearrange("p (b n) -> p b n", b=T)
        hmT = kv[0:RMAX + 1, o + T * RMAX:o + T * RMAX + TOK]
        o += T * RMAX + TOK
        btb_sb = kv[0:RMAX + 1, o:o + D]
        ag_sb = kv[:, o + D:o + D + KT * (RMAX + NR)].rearrange("p (m n) -> p m n", m=KT)
        keyT = kv[:, 0:2 * QUART]
        val = kv[:, 2 * QUART:4 * QUART]
        UW = 3 * D

        def unit_raw(par, which):
            a = 2 * QUART * par + which * UW
            return kv[:, a:a + UW]

        def unit_w(par, part):
            a = (2 * par + part) * UW
            return split[:, :, :].rearrange("p b n -> p (b n)")[:, a:a + UW]

        def unit_h(par, part):
            a = 8192 + (2 * par + part) * TOK
            return split[:, :, :].rearrange("p b n -> p (b n)")[:, a:a + TOK]

        def wbuf(b, part):
            return split[:, b, part * KT * D:(part + 1) * KT * D].rearrange("p (m n) -> p m n", m=KT)

        ctxT_hi = split[:, 2, :].rearrange("p (m n) -> p m n", m=KT)
        ctxT_lo = split[:, 3, :].rearrange("p (m n) -> p m n", m=KT)
        WQ_BUF, WO_BUF = (1, 2), (0, 3)

        def chunk_dst(c, part):
            if c < WK0:
                t = (ctxT_hi, ctxT_lo)[part]
                return t[:, c // 2, (c % 2) * D:(c % 2 + 1) * D]
            if c < WQ0:
                return wbuf(0, part)[:, c - WK0, :]
            if c < WKEY:
                return wbuf(1, part)[:, c - WQ0, :]
            if c < WFFN:
                return wbuf((c - WKEY) // KT, part)[:, c % KT, :]
            if c < WVAL:
                return wbuf(0, part)[:, c - WFFN, :]
            if c < WGRP:
                return wbuf(1 - (c - WVAL) // KT, part)[:, c % KT, :]
            g, k = divmod(c - WGRP, 2 * KT)
            return wbuf((WQ_BUF if k < KT else WO_BUF)[g % 2], part)[:, k % KT, :]

        def as32(ap):
            return ap.bitcast(F32)

        def heads(ap):
            return ap.rearrange("p (h n) -> p h n", h=REP)

        def over(col, n):
            return col.unsqueeze(2).to_broadcast([P, col.shape[1], n])

        def tile(t):
            return slice(t * P, (t + 1) * P)

        ln_buf = (headT, score)

        bank = [stack.enter_context(nc.psum_tensor(f"bank{i}", [P, D], F32)) for i in range(8)]

        s_raw = [sem(f"raw_loaded{i}") for i in range(RING)]
        s_x = [sem("x_loaded0"), sem("x_loaded1")]
        s_ctxn = sem("ctx_loaded")
        s_small = sem("small_loaded")
        s_lora = sem("lora_loaded")
        s_const = sem("const_ready")
        s_wqk = sem("wqk_ready")
        s_hi = sem("chunk_hi")
        s_loc = sem("ctx_chunk_lo")
        s_lo = sem("chunk_lo")
        s_st = sem("ln_stats")
        s_ag = sem("ln_mean_var")
        s_ve = sem("ln_var_eps")
        s_rstd = sem("ln_rstd")
        s_xn = sem("ln_normed")
        s_xt = sem("ln_transposed")
        s_xhi = sem("ln_hi")
        s_xlo = sem("ln_lo")
        s_kq = sem("kq0_product")
        s_kqe = sem("kq0_copied")
        s_sc0 = sem("scores0")
        s_mx0 = sem("max0")
        s_nm0 = sem("negmax0")
        s_ex0 = sem("exp0")
        s_ri0 = sem("rinv0")
        s_pt0 = sem("probs0_transposed")
        s_pe0 = sem("probs0_copied")
        s_pv0 = sem("pv0")
        s_at0 = sem("attended0")
        s_ka = sem("key_product")
        s_ks = sem("key_squares")
        s_km = sem("key_meansq")
        s_kr = sem("key_rms")
        s_kn = sem("key_normed")
        s_kt = sem("key_transposed")
        s_ke = sem("key_copied")
        s_h = sem("lora_down_product")
        s_rt = sem("routing_chain")
        s_ht = sem("lora_transposed")
        s_one = sem("ones_row")
        s_he = sem("lora_copied")
        s_w = sem("ffn0_product")
        s_add = sem("resid_added")
        s_v = sem("value_product")
        s_ve1 = sem("value_copied")
        s_a = sem("q_product")
        s_sq = sem("q_squares")
        s_ms = sem("q_meansq")
        s_rr = sem("q_rms")
        s_qn = sem("q_normed")
        s_b = sem("q_transposed")
        s_qt = sem("q_copied")
        s_c = sem("scores")
        s_sm = sem("masked")
        s_mx = sem("negmax")
        s_ex = sem("exp")
        s_ri = sem("rinv")
        s_pn = sem("probs_normed")
        s_d = sem("probs_transposed")
        s_pt = sem("probs_copied")
        s_e = sem("pv")
        s_ah = sem("attended_hi")
        s_al = sem("attended_lo")
        s_f = sem("out_product")
        s_uw = [sem("unit_loaded0"), sem("unit_loaded1")]
        s_us = sem("unit_zero_sub")
        s_um = sem("unit_scaled")
        s_uha = sem("unit_gateup_hi")
        s_uhb = sem("unit_down_hi")
        s_ula = sem("unit_gateup_lo")
        s_ulb = sem("unit_down_lo")
        s_g = sem("gateup_product")
        s_si = sem("silu")
        s_hm = sem("hidden")
        s_hh = sem("hidden_hi")
        s_hl = sem("hidden_lo")
        s_dn = sem("down_product")
        s_out = sem("stored")

        block = stack.enter_context(nc.Block())

        def lo_done(eng, c):
            if isinstance(c, int) and c < WK0:
                eng.wait_ge(s_loc, c + 1)
            else:
                eng.wait_ge(s_lo, c - WK0 + 1)

        def at(p, k):
            return k if p is None else BODY * p + k

        def unit_at(p, k):
            return k if p is None else 2 * p + k

        @block.sync
        def _(sp):
            def load(c, src):
                if c >= RING:
                    lo_done(sp, c - RING)
                sp.dma_start(raw[:, c % RING, :], src).then_inc(s_raw[c % RING], 16)

            for c in range(WK0):
                load(c, ctxT[c // 2, :, (c % 2) * D:(c % 2 + 1) * D])
            for c in range(WK0, WGRP):
                w, c0 = [(w, c0) for w, c0 in ((wk0, WK0), (wq0, WQ0), (wkey, WKEY), (wffn, WFFN), (wval, WVAL))
                         if c >= c0][-1]
                load(c, w[c - c0])
                if c == WFFN - 1:
                    sp.wait_ge(s_pv0, T)
                    sp.dma_start(ag_sb, agT).then_inc(s_lora, 16)
                    sp.dma_start(btb_sb, bTb).then_inc(s_lora, 16)
            for k in range(2 * KT):
                load(WGRP + k, wqo[k])

            def next_group_chunk(i, p):
                c = WGRP + T + i
                lo_done(sp, WGRP + T + at(p, i) - RING)
                sp.dma_start(raw[:, c % RING, :], wqo[T + i if p is None else BODY * p + (T + i)]).then_inc(s_raw[c % RING], 16)

            for i in range(3):
                next_group_chunk(i, None)
            with sp.Fori(0, STEPS // BODY - 1) as p:
                for j in range(BODY):
                    next_group_chunk(j + 3, p)
            for i in range(STEPS - BODY + 3, STEPS - T):
                next_group_chunk(i, None)

            def load_unit(i, k, par):
                for which, src in ((0, ffn_w[i]), (1, ffn_z[bass.ds(i, 1), :].to_broadcast([P, UW])),
                                   (2, ffn_s[bass.ds(i, 1), :].to_broadcast([P, UW]))):
                    dst = unit_raw(par, which)
                    sp.dma_start(dst if which == 2 else dst.bitcast(I32), src).then_inc(s_uw[par], 16)

            sp.wait_ge(s_c, STEPS)
            load_unit(0, 0, 0)
            sp.wait_ge(s_pt, STEPS)
            load_unit(1, 1, 1)
            with sp.Fori(0, UNITS // 2 - 1) as p:
                for u in range(2):
                    sp.wait_ge(s_ulb, 2 * p + u + 1)
                    load_unit(2 * p + u + 2, u, u)
            for t in range(T):
                sp.wait_ge(s_add, DOWN0 + T * (UNITS - 1) + t + 1)
                sp.dma_start(out[t], resid[:, t, :]).then_inc(s_out, 16)
            sp.wait_ge(s_out, 16 * T)

        @block.gpsimd
        def _(pool):
            pool.memset(ident[:], 0.0).then_inc(s_const, 1)
            pool.memset(mhalf[:], -0.5).then_inc(s_const, 1)
            pool.memset(eps[:], EPS).then_inc(s_const, 1)
            pool.wait_ge(s_const, 1)
            pool.affine_select(out=ident[:], in_=ident[:], compare_op=ALU.not_equal, fill=1.0, base=0,
                               pattern=[[-1, P]], channel_multiplier=1).then_inc(s_const, 1)
            pool.wait_ge(s_const, 4)

            def lo(c, n=None):
                pool.wait_ge(s_hi, (c if n is None else n) + 1)
                pool.tensor_tensor(chunk_dst(c, 1), raw[:, c % RING, :], as32(chunk_dst(c, 0)),
                                   ALU.subtract).then_inc(s_lo, 1)

            def ln_rstd(k, h):
                n, cols = 2 * k + h, slice(HALF * h, HALF * (h + 1))
                pool.wait_ge(s_ag, HALF * (n + 1))
                pool.tensor_tensor(veps[:, cols], mv[:, cols, 1], eps[:, 0:HALF], ALU.add).then_inc(s_ve, 1)
                pool.wait_ge(s_ve, n + 1)
                pool.tensor_tensor(rstd[:, cols], veps[:, cols], mhalf[:, 0:HALF], ALU.pow).then_inc(s_rstd, 1)

            def rms_of(par, n, s_in, s_mid, s_done):
                pool.wait_ge(s_in, n)
                pool.tensor_tensor(msq[:, par, :], ssq[:, par, :], eps[:, 0:REP], ALU.add).then_inc(s_mid, 1)
                pool.wait_ge(s_mid, n)
                pool.tensor_tensor(rms[:, par, :], msq[:, par, :], mhalf[:, 0:REP], ALU.pow).then_inc(s_done, 1)

            ln_rstd(0, 0)
            for c in range(WK0, WK0 + 2):
                lo(c)
            ln_rstd(0, 1)
            for c in range(WK0 + 2, WFFN):
                lo(c)
            for m in range(2 * T):
                rms_of(m % 2, m + 1, s_ks, s_km, s_kr)
                if m in (1, 3):
                    ln_rstd(1, m // 2)
                if m >= 2 * T - KT:
                    lo(WFFN + m - (2 * T - KT))
            for c in range(WVAL, WVAL + 2 * KT):
                lo(c)
            for h in range(2):
                ln_rstd(2, h)
            for c in range(WGRP, WGRP + 2 * KT):
                lo(c)

            def step(j, p):
                if 0 <= j + 3 and (p is not None or j + 3 < STEPS):
                    i = j + 3
                    rms_of(0, at(p, i) + 1, s_sq, s_ms, s_rr)
                    if p is not None or i < STEPS - T:
                        lo(WGRP + T + i, WGRP + T + at(p, i))
                if 0 <= j + 2 and (p is not None or j + 2 < STEPS):
                    i = j + 2
                    pool.wait_ge(s_ri, at(p, i) + 1)
                    pool.tensor_tensor(heads(prob[:]), heads(prob[:]), over(rinv[:, 0:REP], P), ALU.mult)\
                        .then_inc(s_pn, 1)

            for j in range(-3, 0):
                step(j, None)
            with pool.Fori(0, STEPS // BODY - 1) as p:
                for j in range(BODY):
                    step(j, p)
            for j in range(STEPS - BODY, STEPS):
                step(j, None)
                if j == STEPS - 3:
                    ln_rstd(3, 0)
            ln_rstd(3, 1)

            def unit_lo(i, p):
                n, par = unit_at(p, i), i % 2
                pool.wait_ge(s_uha, n + 1)
                pool.tensor_tensor(unit_w(par, 1)[:, 0:2 * D], unit_raw(par, 0)[:, 0:2 * D],
                                   as32(unit_w(par, 0)[:, 0:2 * D]), ALU.subtract).then_inc(s_ula, 1)
                pool.wait_ge(s_uhb, n + 1)
                pool.tensor_tensor(unit_w(par, 1)[:, 2 * D:UW], unit_raw(par, 0)[:, 2 * D:UW],
                                   as32(unit_w(par, 0)[:, 2 * D:UW]), ALU.subtract).then_inc(s_ulb, 1)

            unit_lo(0, None)
            unit_lo(1, None)
            with pool.Fori(0, UNITS // 2 - 1) as p:
                for u in range(2):
                    unit_lo(u + 2, p)

        @block.scalar
        def _(act):
            act.dma_start(resid[:, 0:HALF, :], x[0:HALF].rearrange("b p d -> p b d")).then_inc(s_x[0], 16)
            act.dma_start(resid[:, HALF:T, :], x[HALF:T].rearrange("b p d -> p b d")).then_inc(s_x[1], 16)
            act.dma_start(bias[:], bqk).then_inc(s_small, 16)
            act.dma_start(nw[:], norm_w).then_inc(s_small, 16)
            act.dma_start(mask_sb[:], mask).then_inc(s_small, 16)
            act.dma_start(gb[:], gate_b.to_broadcast([P, NR])).then_inc(s_small, 16)
            act.dma_start(ctxn, ctx.rearrange("b p d -> p b d")).then_inc(s_ctxn, 16)

            def hi(c, p=None, n=None):
                n = c if n is None else n
                turn = c // RING if p is None else c // RING + p * (BODY // RING)
                act.wait_ge(s_raw[c % RING], 16 * (turn + 1))
                act.activation(chunk_dst(c, 0), raw[:, c % RING, :], ACT.Copy).then_inc(s_hi, 1)

            def ln_hi(k, t, keep=False):
                n = T * k + t
                act.wait_ge(s_xt, n + 1)
                src = bank[4 + n % 2][:].rearrange("p (m n) -> p m n", m=KT)
                if keep:
                    act.activation(xnT32[:, :, tile(t)], src, ACT.Copy)
                act.activation(xnT_hi[:, :, tile(t)], src, ACT.Copy).then_inc(s_xhi, 1)

            for c in range(WKEY):
                hi(c)
            act.wait_ge(s_small, 64)
            for n in range(4 * KT):
                m, h = (n % (2 * KT)) // 2, n % 2
                is_q = n // (2 * KT)
                if n == 2 * KT:
                    for t in range(T):
                        ln_hi(0, t)
                    for c in range(WKEY, WKEY + KT):
                        hi(c)
                act.wait_ge(s_kq, n + 1)
                dst = (k0T, q0T)[is_q]
                act.activation(dst[:, m, h * D:(h + 1) * D], bank[n % 4][:], ACT.Identity,
                               bias=bias[:, KT * (1 - is_q) + m:KT * (1 - is_q) + m + 1]).then_inc(s_kqe, 1)
            for c in range(WKEY + KT, WFFN):
                hi(c)
            p0 = norm[:].rearrange("p a n -> p (a n)")
            for b in range(T):
                act.wait_ge(s_nm0, b // HALF + 1)
                act.activation(p0[:, tile(b)], bank[4 + b // HALF][:, tile(b % HALF)], ACT.Exp,
                               bias=nmax[:, b:b + 1], scale=SCALE0, accum_out=rsum[:, b:b + 1]).then_inc(s_ex0, 1)
            for h in range(2):
                act.wait_ge(s_pt0, HALF * (h + 1))
                act.activation((probT, sq)[h][:], bank[6 + h][:], ACT.Copy).then_inc(s_pe0, 1)

            def squares(src, par, s_done):
                for h in range(REP):
                    done = act.activation(sq[:, tile(h)], src[:, tile(h)], ACT.Square, scale=float(P) ** -0.5,
                                          accum_out=ssq[:, par, h:h + 1])
                done.then_inc(s_done, 1)

            act.wait_ge(s_wqk, 1)
            act.wait_ge(s_pv0, T)
            for m in range(2 * T + 2):
                if m < 2 * T:
                    act.wait_ge(s_ka, m + 1)
                    if m >= 2:
                        act.wait_ge(s_kr, m - 1)
                    if m >= 1:
                        act.wait_ge(s_ks, m)
                    squares(bank[m % 2], m % 2, s_ks)
                if 4 <= m < 4 + T:
                    ln_hi(1, m - 4, keep=True)
                if m >= 2:
                    n = m - 2
                    act.wait_ge(s_kt, n + 1)
                    g0 = REP * (n // T)
                    act.activation(keyT.rearrange("p (g n) -> p g n", g=NKV)[:, g0:g0 + REP, tile(n % T)],
                                   heads(bank[2 + n % 2][:]), ACT.Copy, scale=wqk[:, 0:1]).then_inc(s_ke, 1)
                if 2 * T - KT <= m < 2 * T:
                    hi(WFFN + m - (2 * T - KT))
            for c in range(WVAL, WVAL + KT):
                if c == WVAL:
                    act.wait_ge(s_ka, 2 * T)
                hi(c)
            for h in range(2):
                act.wait_ge(s_ht, HALF * (h + 1))
                act.activation(hmT[0:RMAX, h * D:(h + 1) * D], bank[4 + h][0:RMAX, :], ACT.Copy).then_inc(s_he, 1)
            act.wait_ge(s_w, T)
            for c in range(WVAL + KT, WGRP):
                hi(c)
            for m in range(2 * T):
                act.wait_ge(s_v, m + 1)
                vb, t = divmod(m, T)
                act.activation(val[:, t * NKV * P + vb * D:t * NKV * P + (vb + 1) * D], bank[m % 4][:],
                               ACT.Copy).then_inc(s_ve1, 1)
                if 4 <= m < 4 + T:
                    ln_hi(2, m - 4)
                if T + 4 <= m:
                    hi(WGRP + m - T - 4)
            for c in range(WGRP + KT, WGRP + 2 * KT):
                hi(c)

            def step(j, p):
                def valid(k):
                    return 0 <= k and (p is not None or k < STEPS)
                if valid(j + 2):
                    act.wait_ge(s_b, at(p, j + 2) + 1)
                    act.activation(headT[:], bank[1][:], ACT.Copy).then_inc(s_qt, 1)
                if valid(j + 3):
                    act.wait_ge(s_a, at(p, j + 3) + 1)
                    squares(bank[0], 0, s_sq)
                if valid(j + 1):
                    i = j + 1
                    g = i // T if p is None else 2 * p + i // T
                    act.wait_ge(s_e, at(p, i))
                    act.activation(vcur[:], val[:, bass.ds(g * P + (i % T) * NKV * P, P)], ACT.Copy)
                    act.wait_ge(s_d, at(p, i) + 1)
                    act.activation(probT[:], bank[3][:], ACT.Copy).then_inc(s_pt, 1)
                if valid(j + 2):
                    i = j + 2
                    act.wait_ge(s_mx, at(p, i) + 1)
                    act.wait_ge(s_d, at(p, i))
                    for h in range(REP):
                        done = act.activation(prob[:, tile(h)], score[:, tile(h)], ACT.Exp, bias=nmax[:, h:h + 1],
                                              accum_out=rsum[:, h:h + 1])
                    done.then_inc(s_ex, 1)
                if valid(j + 3) and (p is not None or j + 3 < STEPS - T):
                    i = j + 3
                    if i % T == KT:
                        act.wait_ge(s_f, at(p, i - KT) + 1)
                    hi(WGRP + T + i, p)
                if valid(j + 1):
                    act.wait_ge(s_e, at(p, j + 1) + 1)
                    act.activation(aoT_hi[:], bank[6][:], ACT.Copy).then_inc(s_ah, 1)

            for j in range(-3, 0):
                step(j, None)
            with act.Fori(0, STEPS // BODY - 1) as p:
                for j in range(BODY):
                    step(j, p)
            for j in range(STEPS - BODY, STEPS):
                step(j, None)

            def unit_hi(i, p, part):
                n, par = unit_at(p, i), i % 2
                act.wait_ge(s_um, n + 1)
                if part == 0:
                    if i >= 2:
                        act.wait_ge(s_g, 2 * (n - 1))
                    act.activation(unit_w(par, 0)[:, 0:2 * D], unit_raw(par, 0)[:, 0:2 * D], ACT.Copy)\
                        .then_inc(s_uha, 1)
                else:
                    if i >= 2:
                        act.wait_ge(s_dn, T * (n - 1))
                    act.activation(unit_w(par, 0)[:, 2 * D:UW], unit_raw(par, 0)[:, 2 * D:UW], ACT.Copy)\
                        .then_inc(s_uhb, 1)

            def hidden(i, p):
                n, par = unit_at(p, i), i % 2
                for h in range(2):
                    act.wait_ge(s_g, 2 * n + h + 1)
                    if i >= 1:
                        act.wait_ge(s_hm, 2 * (n - 1) + h + 1)
                    act.activation((score, prob)[h][:], bank[2 * h][:], ACT.Silu).then_inc(s_si, 1)
                    act.wait_ge(s_hm, 2 * n + h + 1)
                    act.activation(unit_h(par, 0)[:, h * D:(h + 1) * D], norm[:, h, :], ACT.Copy).then_inc(s_hh, 1)

            unit_hi(0, None, 0)
            unit_hi(0, None, 1)
            for t in range(T):
                ln_hi(3, t)
            unit_hi(1, None, 0)
            hidden(0, None)
            unit_hi(1, None, 1)
            with act.Fori(0, UNITS // 2 - 1) as p:
                for u in range(2):
                    unit_hi(u + 2, p, 0)
                    hidden(u + 1, p)
                    unit_hi(u + 2, p, 1)
            hidden(UNITS - 1, None)

        @block.vector
        def _(dve):
            def ln_stats(k, h):
                for t in range(HALF * h, HALF * (h + 1)):
                    dve.bn_stats(st[:, t, :], resid[:, t, :]).then_inc(s_st, 1)
                for t in range(HALF * h, HALF * (h + 1)):
                    dve.wait_ge(s_st, T * k + t + 1)
                    dve.bn_aggr(mv[:, t, :], st[:, t, :]).then_inc(s_ag, 1)

            def ln_norm(k, t):
                n = T * k + t
                dve.wait_ge(s_rstd, n // HALF + 1)
                if n >= 2:
                    dve.wait_ge(s_xt, n - 1)
                dve.tensor_scalar(ln_buf[n % 2][:], resid[:, t, :], mv[:, t, 0:1], rstd[:, t:t + 1],
                                  ALU.subtract, ALU.mult).then_inc(s_xn, 1)

            def ln_lo(k, t):
                n = T * k + t
                dve.wait_ge(s_xhi, n + 1)
                dve.tensor_tensor(xnT_lo[:, :, tile(t)], bank[4 + n % 2][:].rearrange("p (m n) -> p m n", m=KT),
                                  as32(xnT_hi[:, :, tile(t)]), ALU.subtract).then_inc(s_xlo, 1)

            def ctx_lo(c):
                dve.wait_ge(s_hi, c + 1)
                dve.tensor_tensor(chunk_dst(c, 1), raw[:, c % RING, :], as32(chunk_dst(c, 0)), ALU.subtract)\
                    .then_inc(s_loc, 1)

            for c in range(WK0):
                ctx_lo(c)
                if c in (3, 7):
                    dve.wait_ge(s_x[c // 4], 16)
                    ln_stats(0, c // 4)
            dve.wait_ge(s_small, 64)
            dve.tensor_tensor(wqk[:], nw[:, 0:1], nw[:, 1:2], ALU.mult).then_inc(s_wqk, 1)
            for t in range(T + 1):
                if t < T:
                    ln_norm(0, t)
                if t >= 1:
                    ln_lo(0, t - 1)
            for h in range(2):
                cols = slice(HALF * h, HALF * (h + 1))
                dve.wait_ge(s_sc0, HALF * (h + 1))
                dve.tensor_reduce(rinv[:, cols], heads(bank[4 + h][:]), AX_X, ALU.max).then_inc(s_mx0, 1)
                dve.wait_ge(s_mx0, h + 1)
                dve.tensor_scalar(nmax[:, cols], rinv[:, cols], -SCALE0, None, ALU.mult).then_inc(s_nm0, 1)
            dve.wait_ge(s_nm0, 2)
            for h in range(2):
                cols = slice(HALF * h, HALF * (h + 1))
                dve.wait_ge(s_ex0, HALF * (h + 1))
                dve.reciprocal(rinv[:, cols], rsum[:, cols]).then_inc(s_ri0, 1)
            for b in range(T):
                dve.wait_ge(s_ri0, b // HALF + 1)
                dve.wait_ge(s_pv0, b + 1)
                dve.scalar_tensor_tensor(out=resid[:, b, :], in0=bank[b % 4][:], scalar=rinv[:, b:b + 1],
                                         in1=resid[:, b, :], op0=ALU.mult, op1=ALU.add).then_inc(s_at0, 1)
                if b % HALF == HALF - 1:
                    dve.wait_ge(s_at0, b + 1)
                    ln_stats(1, b // HALF)
            dve.memset(hmT[RMAX:RMAX + 1, :], 1.0).then_inc(s_one, 1)
            for m in range(2 * T + 1):
                if 2 <= m < 2 + T:
                    ln_norm(1, m - 2)
                if m >= 1:
                    n = m - 1
                    dve.wait_ge(s_kr, n + 1)
                    if n >= 2:
                        dve.wait_ge(s_kt, n - 1)
                    dve.tensor_tensor(heads(norm[:, n % 2, :]), heads(bank[n % 2][:]), over(rms[:, n % 2, :], P),
                                      ALU.mult).then_inc(s_kn, 1)
                if 4 <= m < 4 + T:
                    ln_lo(1, m - 4)
            for h in range(2):
                cols = slice(HALF * h, HALF * (h + 1))
                src = bank[6 + h][:, 0:HALF * (RMAX + NR)].rearrange("p (b n) -> p b n", b=HALF)
                dve.wait_ge(s_h, HALF * (h + 1))
                dve.tensor_copy(hs[:, cols, :], src[:, :, 0:RMAX])
                dve.tensor_tensor(sc[:, cols, :], src[:, :, RMAX:RMAX + NR],
                                  gb[:].unsqueeze(1).to_broadcast([P, HALF, NR]), ALU.add).then_inc(s_rt, 1)
            dve.wait_ge(s_rt, 2)
            dve.tensor_copy(pmax[:, :, 0], sc[:, :, 0]).then_inc(s_rt, 1)
            for r in range(1, NR):
                dve.wait_ge(s_rt, 2 + r)
                dve.tensor_tensor(pmax[:, :, r], pmax[:, :, r - 1], sc[:, :, r], ALU.max).then_inc(s_rt, 1)
            dve.wait_ge(s_rt, 2 + NR)
            dve.tensor_tensor(ind[:], pmax[:, :, 0:NR - 1],
                              pmax[:, :, NR - 1:NR].to_broadcast([P, T, NR - 1]), ALU.is_lt).then_inc(s_rt, 1)
            dve.wait_ge(s_rt, 3 + NR)
            for r in range(1, NR):
                rows = slice(RANKS[r - 1], RANKS[r])
                dve.tensor_tensor(hs[:, :, rows], hs[:, :, rows],
                                  ind[:, :, r - 1:r].to_broadcast([P, T, RANKS[r] - RANKS[r - 1]]), ALU.mult)\
                    .then_inc(s_rt, 1)
            for t in range(T):
                dve.wait_ge(s_w, t + 1)
                dve.tensor_tensor(resid[:, t, :], bank[t % 4][:], resid[:, t, :], ALU.add).then_inc(s_add, 1)
                if t % HALF == HALF - 1:
                    dve.wait_ge(s_add, t + 1)
                    ln_stats(2, t // HALF)
            for t in range(T + 1):
                if t < T:
                    ln_norm(2, t)
                if t >= 1:
                    ln_lo(2, t - 1)

            def step(j, p):
                def valid(k):
                    return 0 <= k and (p is not None or k < STEPS)
                if valid(j + 2):
                    i = j + 2
                    dve.wait_ge(s_c, at(p, i) + 1)
                    dve.wait_ge(s_ex, at(p, i))
                    dve.scalar_tensor_tensor(out=heads(score[:]), in0=heads(bank[2][:]), scalar=SCALE1,
                                             in1=mask_sb[:].unsqueeze(1).to_broadcast([P, REP, P]),
                                             op0=ALU.mult, op1=ALU.add).then_inc(s_sm, 1)
                    dve.wait_ge(s_sm, at(p, i) + 1)
                    dve.tensor_reduce(nmax[:, 0:REP], heads(score[:]), AX_X, ALU.max, negate=True)\
                        .then_inc(s_mx, 1)
                if valid(j + 3):
                    i = j + 3
                    dve.wait_ge(s_rr, at(p, i) + 1)
                    dve.tensor_tensor(heads(norm[:, 0, :]), heads(bank[0][:]), over(rms[:, 0, :], P), ALU.mult)\
                        .then_inc(s_qn, 1)
                if valid(j + 2):
                    dve.wait_ge(s_ex, at(p, j + 2) + 1)
                    dve.reciprocal(rinv[:, 0:REP], rsum[:, 0:REP]).then_inc(s_ri, 1)
                if valid(j):
                    dve.wait_ge(s_f, at(p, j) + 1)
                    dve.tensor_tensor(resid[:, j % T, :], bank[7][:], resid[:, j % T, :], ALU.add)\
                        .then_inc(s_add, 1)
                if valid(j + 1):
                    dve.wait_ge(s_ah, at(p, j + 1) + 1)
                    dve.tensor_tensor(aoT_lo[:], bank[6][:], as32(aoT_hi[:]), ALU.subtract).then_inc(s_al, 1)

            for j in range(-3, 0):
                step(j, None)
            with dve.Fori(0, STEPS // BODY - 1) as p:
                for j in range(BODY):
                    step(j, p)
            for j in range(STEPS - BODY, STEPS):
                step(j, None)
                if j == STEPS - HALF - 1:
                    dve.wait_ge(s_add, T + j + 1)
                    ln_stats(3, 0)

            def dequant(i, p):
                n, par = unit_at(p, i), i % 2
                turn = n // 2 if p is None else p + i // 2
                dve.wait_ge(s_uw[par], 48 * (turn + 1))
                w, z, s = (unit_raw(par, k) for k in range(3))
                dve.tensor_tensor(z, w.bitcast(I32), z.bitcast(I32), ALU.subtract).then_inc(s_us, 1)
                dve.wait_ge(s_us, n + 1)
                dve.tensor_tensor(w, z, s, ALU.mult).then_inc(s_um, 1)

            def hidden(i, p):
                n, par = unit_at(p, i), i % 2
                for h in range(2):
                    dve.wait_ge(s_si, 2 * n + h + 1)
                    if i >= 1:
                        dve.wait_ge(s_hl, 2 * (n - 1) + h + 1)
                    dve.tensor_tensor(norm[:, h, :], (score, prob)[h][:], bank[2 * h + 1][:], ALU.mult)\
                        .then_inc(s_hm, 1)
                    dve.wait_ge(s_hh, 2 * n + h + 1)
                    dve.tensor_tensor(unit_h(par, 1)[:, h * D:(h + 1) * D], norm[:, h, :],
                                      as32(unit_h(par, 0)[:, h * D:(h + 1) * D]), ALU.subtract).then_inc(s_hl, 1)

            def add_down(i, p):
                n = unit_at(p, i)
                for t in range(T):
                    dve.wait_ge(s_dn, T * n + t + 1)
                    dve.tensor_tensor(resid[:, t, :], bank[4 + t % 4][:], resid[:, t, :], ALU.add).then_inc(s_add, 1)

            dve.wait_ge(s_add, T + STEPS)
            ln_stats(3, 1)
            dequant(0, None)
            for t in range(T + 1):
                if t < T:
                    ln_norm(3, t)
                if t >= 1:
                    ln_lo(3, t - 1)
            dequant(1, None)
            hidden(0, None)
            with dve.Fori(0, UNITS // 2 - 1) as p:
                for u in range(2):
                    dve.wait_ge(s_ulb, 2 * p + u + 1)
                    dequant(u + 2, p)
                    hidden(u + 1, p)
                    add_down(u, p)
            hidden(UNITS - 1, None)
            add_down(UNITS - 2, None)
            add_down(UNITS - 1, None)

        @block.tensor
        def _(pe):
            def three(dst, l_hi, l_lo, r_hi, r_lo, first, last):
                pe.matmul(dst, l_hi, r_hi, start=first, stop=False)
                pe.matmul(dst, l_hi, r_lo, start=False, stop=False)
                return pe.matmul(dst, l_lo, r_hi, start=False, stop=last)

            def ln_transpose(k, t):
                n = T * k + t
                pe.wait_ge(s_xn, n + 1)
                if n >= 2:
                    pe.wait_ge(s_xlo, n - 1)
                for m in range(KT):
                    done = pe.transpose(bank[4 + n % 2][:, tile(m)], ln_buf[n % 2][:, tile(m)], ident[:])
                done.then_inc(s_xt, 1)

            pe.wait_ge(s_const, 4)
            for n in range(4 * KT):
                m, h = (n % (2 * KT)) // 2, n % 2
                is_q = n // (2 * KT)
                if n == 0:
                    lo_done(pe, WK0 - 1)
                    lo_done(pe, WQ0 - 1)
                if n == 2 * KT:
                    for t in range(T):
                        ln_transpose(0, t)
                    lo_done(pe, WKEY - 1)
                    pe.wait_ge(s_xlo, T)
                if n >= 4:
                    pe.wait_ge(s_kqe, n - 3)
                r_hi, r_lo = ((ctxT_hi, ctxT_lo), (xnT_hi, xnT_lo))[is_q]
                for k in range(KT):
                    done = three(bank[n % 4][:], wbuf(is_q, 0)[:, k, tile(m)], wbuf(is_q, 1)[:, k, tile(m)],
                                 r_hi[:, k, h * D:(h + 1) * D], r_lo[:, k, h * D:(h + 1) * D],
                                 k == 0, k == KT - 1)
                done.then_inc(s_kq, 1)
            pe.wait_ge(s_kqe, 4 * KT)
            for b in range(T):
                for m in range(KT):
                    done = pe.matmul(bank[4 + b // HALF][:, tile(b % HALF)], q0T[:, m, tile(b)], k0T[:, m, tile(b)],
                                     start=(m == 0), stop=(m == KT - 1))
                done.then_inc(s_sc0, 1)
            p0 = norm[:].rearrange("p a n -> p (a n)")
            for b in range(T):
                pe.wait_ge(s_ex0, b + 1)
                pe.transpose(bank[6 + b // HALF][:, tile(b % HALF)], p0[:, tile(b)], ident[:]).then_inc(s_pt0, 1)
            pe.wait_ge(s_ctxn, 16)
            for b in range(T):
                pe.wait_ge(s_pe0, b // HALF + 1)
                if b >= 4:
                    pe.wait_ge(s_at0, b - 3)
                pe.matmul(bank[b % 4][:], (probT, sq)[b // HALF][:, tile(b % HALF)], ctxn[:, b, :],
                          start=True, stop=True).then_inc(s_pv0, 1)
            for m in range(2 * T + 2):
                if m < 2 * T:
                    kb, t = divmod(m, T)
                    if t == 0:
                        lo_done(pe, WKEY + KT * (kb + 1) - 1)
                    if m == 0:
                        pe.wait_ge(s_at0, T)
                    if m >= 2:
                        pe.wait_ge(s_kn, m - 1)
                    for k in range(KT):
                        done = three(bank[m % 2][:], ctxT_hi[:, k, tile(t)], ctxT_lo[:, k, tile(t)],
                                     wbuf(kb, 0)[:, k, :], wbuf(kb, 1)[:, k, :], k == 0, k == KT - 1)
                    done.then_inc(s_ka, 1)
                if 3 <= m < 3 + T:
                    ln_transpose(1, m - 3)
                if m >= 2:
                    n = m - 2
                    pe.wait_ge(s_kn, n + 1)
                    if n >= 2:
                        pe.wait_ge(s_ke, n - 1)
                    for h in range(REP):
                        done = pe.transpose(bank[2 + n % 2][:, tile(h)], norm[:, n % 2, tile(h)], ident[:])
                    done.then_inc(s_kt, 1)
            pe.wait_ge(s_lora, 32)
            pe.wait_ge(s_xlo, 2 * T)
            for t in range(T):
                for k in range(KT):
                    c = (t % HALF) * (RMAX + NR)
                    done = pe.matmul(bank[6 + t // HALF][:, c:c + RMAX + NR], xnT32[:, k, tile(t)], ag_sb[:, k, :],
                                     start=(k == 0), stop=(k == KT - 1))
                done.then_inc(s_h, 1)

            def dense(t):
                for k in range(KT):
                    three(bank[t % 4][:], xnT_hi[:, k, tile(t)], xnT_lo[:, k, tile(t)],
                          wbuf(0, 0)[:, k, :], wbuf(0, 1)[:, k, :], k == 0, False)

            def routed(t):
                pe.matmul(bank[t % 4][:], hmT[:, tile(t)], btb_sb, start=False, stop=True).then_inc(s_w, 1)

            lo_done(pe, WVAL - 1)
            pe.wait_ge(s_ke, 2 * T)
            for t in range(HALF):
                dense(t)
            pe.wait_ge(s_rt, 3 + NR + NR - 1)
            for t in range(T):
                pe.transpose(bank[4 + t // HALF][0:RMAX, tile(t % HALF)], hs[:, t, :], ident[:]).then_inc(s_ht, 1)
            pe.wait_ge(s_he, 2)
            pe.wait_ge(s_one, 1)
            for t in range(HALF):
                routed(t)
            for t in range(HALF, T):
                pe.wait_ge(s_add, t - HALF + 1)
                dense(t)
                routed(t)
            for m in range(2 * T):
                vb, t = divmod(m, T)
                if t == 0:
                    lo_done(pe, WVAL + KT * (vb + 1) - 1)
                if m < 4:
                    pe.wait_ge(s_add, HALF + m + 1)
                else:
                    pe.wait_ge(s_ve1, m - 3)
                for k in range(KT):
                    done = three(bank[m % 4][:], ctxT_hi[:, k, tile(t)], ctxT_lo[:, k, tile(t)],
                                 wbuf(1 - vb, 0)[:, k, :], wbuf(1 - vb, 1)[:, k, :], k == 0, k == KT - 1)
                done.then_inc(s_v, 1)
                if 3 <= m < 3 + T:
                    ln_transpose(2, m - 3)
            pe.wait_ge(s_ve1, 2 * T)
            pe.wait_ge(s_xlo, 3 * T)

            def step(j, p):
                def valid(k):
                    return 0 <= k and (p is not None or k < STEPS)
                if valid(j + 2):
                    n = at(p, j + 2)
                    pe.wait_ge(s_qn, n + 1)
                    pe.wait_ge(s_qt, n)
                    for h in range(REP):
                        done = pe.transpose(bank[1][:, tile(h)], norm[:, 0, tile(h)], ident[:])
                    done.then_inc(s_b, 1)
                if valid(j + 3):
                    i = j + 3
                    n, t = at(p, i), i % T
                    if t == 0:
                        lo_done(pe, WGRP + n + KT - 1)
                    pe.wait_ge(s_qn, n)
                    b = WQ_BUF[i // T % 2]
                    for k in range(KT):
                        done = three(bank[0][:], xnT_hi[:, k, tile(t)], xnT_lo[:, k, tile(t)],
                                     wbuf(b, 0)[:, k, :], wbuf(b, 1)[:, k, :], k == 0, k == KT - 1)
                    done.then_inc(s_a, 1)
                if valid(j + 2):
                    i = j + 2
                    n, t = at(p, i), i % T
                    g = i // T if p is None else 2 * p + i // T
                    pe.wait_ge(s_qt, n + 1)
                    pe.wait_ge(s_sm, n)
                    for h in range(REP):
                        done = pe.matmul(bank[2][:, tile(h)], headT[:, tile(h)],
                                         keyT[:, bass.ds(g * TOK + t * P, P)], start=True, stop=True)
                    done.then_inc(s_c, 1)
                if valid(j + 1):
                    n = at(p, j + 1)
                    pe.wait_ge(s_pn, n + 1)
                    pe.wait_ge(s_pt, n)
                    for h in range(REP):
                        done = pe.transpose(bank[3][:, tile(h)], prob[:, tile(h)], ident[:])
                    done.then_inc(s_d, 1)
                if valid(j):
                    n, t = at(p, j), j % T
                    if t == 0:
                        lo_done(pe, WGRP + n + 2 * KT - 1)
                    pe.wait_ge(s_al, n + 1)
                    pe.wait_ge(s_add, T + n)
                    b = WO_BUF[j // T % 2]
                    for h in range(REP):
                        done = three(bank[7][:], aoT_hi[:, tile(h)], aoT_lo[:, tile(h)],
                                     wbuf(b, 0)[:, h, :], wbuf(b, 1)[:, h, :], h == 0, h == REP - 1)
                    done.then_inc(s_f, 1)
                if valid(j + 1):
                    n = at(p, j + 1)
                    pe.wait_ge(s_pt, n + 1)
                    pe.wait_ge(s_al, n)
                    pe.matmul(bank[6][:], vcur[:], probT[:], start=True, stop=True).then_inc(s_e, 1)

            for j in range(-3, 0):
                step(j, None)
            with pe.Fori(0, STEPS // BODY - 1) as p:
                for j in range(BODY):
                    step(j, p)
            for j in range(STEPS - BODY, STEPS):
                step(j, None)

            for t in range(T):
                ln_transpose(3, t)

            def gate_up(i, p):
                n, par = unit_at(p, i), i % 2
                pe.wait_ge(s_ula, n + 1)
                for h in range(2):
                    if i >= 1:
                        pe.wait_ge(s_hm, 2 * (n - 1) + h + 1)
                    if i == 0:
                        pe.wait_ge(s_xlo, 3 * T + HALF * (h + 1))
                    for u in range(2):
                        for k in range(KT):
                            cols = slice(u * D + k * P, u * D + (k + 1) * P)
                            done = three(bank[2 * h + u][:], unit_w(par, 0)[:, cols], unit_w(par, 1)[:, cols],
                                         xnT_hi[:, k, h * D:(h + 1) * D], xnT_lo[:, k, h * D:(h + 1) * D],
                                         k == 0, k == KT - 1)
                    done.then_inc(s_g, 1)

            def down(i, p):
                n, par = unit_at(p, i), i % 2
                pe.wait_ge(s_ulb, n + 1)
                pe.wait_ge(s_hl, 2 * n + 2)
                for t in range(T):
                    if t >= 4:
                        pe.wait_ge(s_add, DOWN0 + T * n + t - 3)
                    else:
                        pe.wait_ge(s_add, DOWN0 + T * n)
                    three(bank[4 + t % 4][:], unit_h(par, 0)[:, tile(t)], unit_h(par, 1)[:, tile(t)],
                          unit_w(par, 0)[:, 2 * D:UW], unit_w(par, 1)[:, 2 * D:UW], True, True).then_inc(s_dn, 1)

            gate_up(0, None)
            with pe.Fori(0, UNITS // 2 - 1) as p:
                for u in range(2):
                    gate_up(u + 1, p)
                    down(u, p)
            gate_up(UNITS - 1, None)
            down(UNITS - 2, None)
            down(UNITS - 1, None)


def _program(nc, shapes):
    args = {n: nc.dram_tensor(f"in_{n}_dram", s, d, kind="ExternalInput").ap() for n, s, d in shapes}
    args["out"] = nc.dram_tensor("out_0_dram", (T, P, D), F32, kind="ExternalOutput").ap()
    cross_attention_ffn(nc, **args)


def kernel(**inputs):
    import numpy as np
    import concourse.bacc as bacc
    from concourse.bass_utils import run_bass_kernel_spmd

    a = {k: np.asarray(v) for k, v in inputs.items()}

    def rows(w):
        return w.T

    def blocks(w, n):
        return w.reshape(-1, P, w.shape[1] // n, n).transpose(2, 0, 1, 3)

    def units(w):
        return w.reshape(KT, P, UNITS, P).transpose(2, 1, 0, 3).reshape(UNITS, P, D)

    def unit_rows(w):
        return w.reshape(KT, UNITS, P).transpose(1, 0, 2).reshape(UNITS, D)

    laid = {
        "x": a["x"],
        "ctx": a["ctx_4096"],
        "ctxT": a["ctx_4096"].reshape(TOK, D).T.reshape(KT, P, TOK),
        "wk0": rows(a["L0_xattn_Wk"]).reshape(KT, P, D),
        "wq0": rows(a["L0_xattn_Wq"]).reshape(KT, P, D),
        "bqk": np.concatenate([a["L0_xattn_bq"].reshape(KT, P).T, a["L0_xattn_bk"].reshape(KT, P).T], 1),
        "wkey": blocks(rows(a["L1_xattn_k_proj_w"]), D).reshape(2 * KT, P, D),
        "wffn": rows(a["L0_ffn_W"]).reshape(KT, P, D),
        "wval": blocks(rows(a["L1_xattn_v_proj_w"]), D).reshape(2 * KT, P, D),
        "agT": rows(np.concatenate([a["L0_ffn_A"], a["L0_ffn_gate_w"]], 0))
            .reshape(KT, P, RMAX + NR).transpose(1, 0, 2),
        "bTb": np.concatenate([rows(a["L0_ffn_B"]), a["L0_ffn_b"][None]], 0),
        "gate_b": a["L0_ffn_gate_b"][None],
        "norm_w": np.stack([a["L1_xattn_q_norm_w"], a["L1_xattn_k_norm_w"]], 1),
        "mask": a["mask_1x1xSxS2_ff0"][0, 0],
        "wqo": np.concatenate([blocks(rows(a["L1_xattn_q_proj_w"]), D),
                               rows(a["L1_xattn_o_proj_w"]).reshape(NKV, REP, P, D)], 1).reshape(-1, P, D),
        "ffn_w": np.concatenate([units(a["L1_ffn_gate_w"]), units(a["L1_ffn_up_w"]),
                                 a["L1_ffn_down_w"].reshape(UNITS, P, D)], 2),
        "ffn_z": np.concatenate([unit_rows(a["L1_ffn_gate_z"]), unit_rows(a["L1_ffn_up_z"]),
                                 a["L1_ffn_down_z"]], 1),
        "ffn_s": np.concatenate([unit_rows(a["L1_ffn_gate_s"]), unit_rows(a["L1_ffn_up_s"]),
                                 a["L1_ffn_down_s"]], 1),
    }
    laid = {k: np.ascontiguousarray(v) for k, v in laid.items()}
    nc = bacc.Bacc("TRN2", target_bir_lowering=False, num_devices=1)
    _program(nc, [(k, v.shape, mybir.dt.from_np(v.dtype)) for k, v in laid.items()])
    r = run_bass_kernel_spmd(nc, [{f"in_{k}_dram": v for k, v in laid.items()}], core_ids=[0])
    return r.results[0]["out_0_dram"]
```

```python
from contextlib import ExitStack

import concourse.bass as bass
from concourse import mybir

F32 = mybir.dt.float32
F32R = mybir.dt.float32r
I32 = mybir.dt.int32
ALU = mybir.AluOpType
ACT = mybir.ActivationFunctionType
AX_X = mybir.AxisListType.X

P = 128
T = 8
HALF = T // 2
D = 512
KT = D // P
TOK = T * P
NKV = 8
REP = 4
RANKS = (8, 16, 32, 64)
RMAX = RANKS[-1]
NR = len(RANKS)
F = 1792
UNITS = F // P
EPS = 1e-5
SCALE0 = 1.0 / float(D) ** 0.5
SCALE1 = 1.0 / float(P) ** 0.5

RING = 4
FIRST = 8
WQ0, WKEY, WFFN, WVAL = 12, 16, 24, 28
WGRP = 36
STEPS = NKV * T
DOWN0 = T + STEPS
BODY = 2 * T


def cross_attention_ffn(nc, x, ctx, ctxT, wk0, wq0, bqk, wkey, wffn, wval, agT, bTb, gate_b, norm_w, mask,
                        wqo, ffn_w, ffn_z, ffn_s, out):
    with ExitStack() as stack:
        def sb(name, shape, dt=F32):
            return stack.enter_context(nc.sbuf_tensor(name, shape, dt))

        def sem(name):
            return stack.enter_context(nc.semaphore(name))

        resid = sb("resid", [P, T, D])
        xnT_hi = sb("xnT_hi", [P, KT, TOK], F32R)
        xnT_lo = sb("xnT_lo", [P, KT, TOK], F32R)
        split = sb("split", [P, 4, 2 * KT * D], F32R)
        kv = sb("kv", [P, 2 * T * KT * 2 * P])
        raw = sb("raw", [P, RING, D])
        sq = sb("sq", [P, D])
        norm = sb("norm", [P, 2, D])
        headT = sb("headT", [P, D])
        score = sb("score", [P, D])
        prob = sb("prob", [P, D])
        probT_hi = sb("probT_hi", [P, D], F32R)
        probT_lo = sb("probT_lo", [P, D], F32R)
        aoT_hi = sb("aoT_hi", [P, D], F32R)
        aoT_lo = sb("aoT_lo", [P, D], F32R)
        vcur_hi = sb("vcur_hi", [P, P], F32R)
        vcur_lo = sb("vcur_lo", [P, P], F32R)
        ident = sb("ident", [P, P])
        mask_sb = sb("mask_sb", [P, P])
        mhalf = sb("mhalf", [P, T])
        eps = sb("eps", [P, T])
        bias = sb("bias", [P, 2 * KT])
        nw = sb("nw", [P, 2])
        wqk = sb("wqk", [P, 1])
        gb = sb("gb", [P, NR])
        st = sb("st", [P, T, 6])
        mv = sb("mv", [P, T, 2])
        veps = sb("veps", [P, T])
        rstd = sb("rstd", [P, T])
        ssq = sb("ssq", [P, 2, REP])
        msq = sb("msq", [P, 2, REP])
        rms = sb("rms", [P, 2, REP])
        nmax = sb("nmax", [P, T])
        rsum = sb("rsum", [P, T])
        rinv = sb("rinv", [P, T])
        sc = sb("sc", [P, T, NR])
        pmax = sb("pmax", [P, T, NR])
        ind = sb("ind", [P, T, NR - 1])

        QUART = KT * TOK
        q0T = kv[:, 0:QUART].rearrange("p (m n) -> p m n", m=KT)
        k0T = kv[:, QUART:2 * QUART].rearrange("p (m n) -> p m n", m=KT)
        ctxn = kv[:, 2 * QUART:3 * QUART].rearrange("p (b n) -> p b n", b=T)
        xnT32 = kv[:, 3 * QUART:4 * QUART].rearrange("p (m n) -> p m n", m=KT)
        o = 2 * QUART
        hs = kv[:, o:o + T * RMAX].rearrange("p (b n) -> p b n", b=T)
        hmT = kv[0:RMAX + 1, o + T * RMAX:o + T * RMAX + TOK]
        o += T * RMAX + TOK
        btb_sb = kv[0:RMAX + 1, o:o + D]
        ag_sb = kv[:, o + D:o + D + KT * (RMAX + NR)].rearrange("p (m n) -> p m n", m=KT)
        keyT = kv[:, 0:2 * QUART]
        val = kv[:, 2 * QUART:4 * QUART]
        UW = 3 * D

        def unit_raw(par, which):
            a = (3 * par + which) * UW
            return kv[:, a:a + UW]

        def unit_w(par, part):
            a = (2 * par + part) * UW
            return split[:, :, :].rearrange("p b n -> p (b n)")[:, a:a + UW]

        def unit_h(par, part):
            a = 8192 + (2 * par + part) * TOK
            return split[:, :, :].rearrange("p b n -> p (b n)")[:, a:a + TOK]

        def wbuf(b, part):
            return split[:, b, part * KT * D:(part + 1) * KT * D].rearrange("p (m n) -> p m n", m=KT)

        ctxT_hi = split[:, 2, :].rearrange("p (m n) -> p m n", m=KT)
        ctxT_lo = split[:, 3, :].rearrange("p (m n) -> p m n", m=KT)
        KQ_BANK = (0, 1, 2, 3, 6, 7)
        WQ_BUF, WO_BUF = (1, 2), (0, 3)

        def chunk_dst(c, part):
            if c < WQ0:
                k, h = c // 3, c % 3 - 1
                if h < 0:
                    return wbuf(0, part)[:, k, :]
                return (ctxT_hi, ctxT_lo)[part][:, k, h * D:(h + 1) * D]
            if c < WKEY:
                return wbuf(1, part)[:, c - WQ0, :]
            if c < WFFN:
                return wbuf((c - WKEY) // KT, part)[:, c % KT, :]
            if c < WVAL:
                return wbuf(0, part)[:, c - WFFN, :]
            if c < WGRP:
                return wbuf(1 - (c - WVAL) // KT, part)[:, c % KT, :]
            g, k = divmod(c - WGRP, 2 * KT)
            return wbuf((WQ_BUF if k < KT else WO_BUF)[g % 2], part)[:, k % KT, :]

        def chunk_raw(c):
            if c < FIRST:
                return kv[:, 3 * QUART + c * D:3 * QUART + (c + 1) * D]
            return raw[:, c % RING, :]

        def as32(ap):
            return ap.bitcast(F32)

        def heads(ap):
            return ap.rearrange("p (h n) -> p h n", h=REP)

        def over(col, n):
            return col.unsqueeze(2).to_broadcast([P, col.shape[1], n])

        def tile(t):
            return slice(t * P, (t + 1) * P)

        ln_buf = (headT, score)

        bank = [stack.enter_context(nc.psum_tensor(f"bank{i}", [P, D], F32)) for i in range(8)]

        s_first = [sem(f"first_loaded{i}") for i in range(FIRST)]
        s_raw = [sem(f"raw_loaded{i}") for i in range(RING)]
        s_x = [sem("x_loaded0"), sem("x_loaded1")]
        s_ctxn = sem("ctx_loaded")
        s_small = sem("small_loaded")
        s_lora = sem("lora_loaded")
        s_const = sem("const_ready")
        s_wqk = sem("wqk_ready")
        s_hi = sem("chunk_hi")
        s_loc = sem("ctx_chunk_lo")
        s_lo = sem("chunk_lo")
        s_st = sem("ln_stats")
        s_ag = sem("ln_mean_var")
        s_ve = sem("ln_var_eps")
        s_rstd = sem("ln_rstd")
        s_xn = sem("ln_normed")
        s_xt = sem("ln_transposed")
        s_xhi = sem("ln_hi")
        s_xlo = sem("ln_lo")
        s_kq = sem("kq0_product")
        s_kqe = sem("kq0_copied")
        s_sc0 = sem("scores0")
        s_mx0 = sem("max0")
        s_nm0 = sem("negmax0")
        s_ex0 = sem("exp0")
        s_ri0 = sem("rinv0")
        s_pt0 = sem("probs0_transposed")
        s_pe0 = sem("probs0_copied")
        s_pv0 = sem("pv0")
        s_at0 = sem("attended0")
        s_ka = sem("key_product")
        s_ks = sem("key_squares")
        s_km = sem("key_meansq")
        s_kr = sem("key_rms")
        s_kn = sem("key_normed")
        s_kt = sem("key_transposed")
        s_ke = sem("key_copied")
        s_h = sem("lora_down_product")
        s_rt = sem("routing_chain")
        s_ht = sem("lora_transposed")
        s_one = sem("ones_row")
        s_he = sem("lora_copied")
        s_w = sem("ffn0_product")
        s_add = sem("resid_added")
        s_v = sem("value_product")
        s_ve1 = sem("value_copied")
        s_a = sem("q_product")
        s_sq = sem("q_squares")
        s_ms = sem("q_meansq")
        s_rr = sem("q_rms")
        s_qn = sem("q_normed")
        s_b = sem("q_transposed")
        s_qt = sem("q_copied")
        s_c = sem("scores")
        s_sm = sem("masked")
        s_mx = sem("negmax")
        s_ex = sem("exp")
        s_ri = sem("rinv")
        s_pn = sem("probs_normed")
        s_d = sem("probs_transposed")
        s_pt = sem("probs_copied")
        s_ptl = sem("probs_lo")
        s_vh = sem("step_values_hi")
        s_vl = sem("step_values_lo")
        s_e = sem("pv")
        s_ah = sem("attended_hi")
        s_al = sem("attended_lo")
        s_f = sem("out_product")
        s_uw = [sem("unit_loaded0"), sem("unit_loaded1")]
        s_us = sem("unit_zero_sub")
        s_um = sem("unit_scaled")
        s_uha = sem("unit_gateup_hi")
        s_uhb = sem("unit_down_hi")
        s_ula = sem("unit_gateup_lo")
        s_ulb = sem("unit_down_lo")
        s_g = sem("gateup_product")
        s_si = sem("silu")
        s_hm = sem("hidden")
        s_hh = sem("hidden_hi")
        s_hl = sem("hidden_lo")
        s_dn = sem("down_product")
        s_out = sem("stored")

        block = stack.enter_context(nc.Block())

        def lo_done(eng, c):
            if isinstance(c, int) and c < WQ0 and c % 3:
                eng.wait_ge(s_loc, c - c // 3)
            elif isinstance(c, int) and c < WQ0:
                eng.wait_ge(s_lo, c // 3 + 1)
            else:
                eng.wait_ge(s_lo, c - WQ0 + KT + 1)

        def at(p, k):
            return k if p is None else BODY * p + k

        def unit_at(p, k):
            return k if p is None else 2 * p + k

        @block.sync
        def _(sp):
            def load(c, src):
                if c >= FIRST + RING:
                    lo_done(sp, c - RING)
                sp.dma_start(chunk_raw(c), src).then_inc(s_first[c] if c < FIRST else s_raw[c % RING], 16)

            for k in range(KT):
                load(3 * k, wk0[k])
                for h in range(2):
                    load(3 * k + 1 + h, ctxT[k, :, h * D:(h + 1) * D])
            for c in range(WQ0, WGRP):
                w, c0 = [(w, c0) for w, c0 in ((wq0, WQ0), (wkey, WKEY), (wffn, WFFN), (wval, WVAL))
                         if c >= c0][-1]
                load(c, w[c - c0])
                if c == WKEY - 1:
                    sp.dma_start(ctxn, ctx.rearrange("b p d -> p b d")).then_inc(s_ctxn, 16)
                if c == WFFN - 1:
                    sp.wait_ge(s_pv0, T)
                    sp.dma_start(ag_sb, agT).then_inc(s_lora, 16)
                    sp.dma_start(btb_sb, bTb).then_inc(s_lora, 16)
            for k in range(2 * KT):
                load(WGRP + k, wqo[k])

            def next_group_chunk(i, p):
                c = WGRP + T + i
                lo_done(sp, WGRP + T + at(p, i) - RING)
                sp.dma_start(raw[:, c % RING, :], wqo[T + i if p is None else BODY * p + (T + i)]).then_inc(s_raw[c % RING], 16)

            for i in range(3):
                next_group_chunk(i, None)
            with sp.Fori(0, STEPS // BODY - 1) as p:
                for j in range(BODY):
                    next_group_chunk(j + 3, p)
            for i in range(STEPS - BODY + 3, STEPS - T):
                next_group_chunk(i, None)

            def load_unit(i, k, par):
                for which, src in ((0, ffn_w[i]), (1, ffn_z[bass.ds(i, 1), :].to_broadcast([P, UW])),
                                   (2, ffn_s[bass.ds(i, 1), :].to_broadcast([P, UW]))):
                    dst = unit_raw(par, which)
                    sp.dma_start(dst if which == 2 else dst.bitcast(I32), src).then_inc(s_uw[par], 16)

            sp.wait_ge(s_c, 6 * T)
            load_unit(0, 0, 0)
            sp.wait_ge(s_c, STEPS)
            sp.wait_ge(s_vl, STEPS - T + 1)
            load_unit(1, 1, 1)
            with sp.Fori(0, UNITS // 2 - 1) as p:
                for u in range(2):
                    sp.wait_ge(s_ulb, 2 * p + u + 1)
                    load_unit(2 * p + u + 2, u, u)
            for t in range(T):
                sp.wait_ge(s_add, DOWN0 + T * (UNITS - 1) + t + 1)
                sp.dma_start(out[t], resid[:, t, :]).then_inc(s_out, 16)
            sp.wait_ge(s_out, 16 * T)

        @block.gpsimd
        def _(pool):
            pool.memset(ident[:], 0.0).then_inc(s_const, 1)
            pool.memset(mhalf[:], -0.5).then_inc(s_const, 1)
            pool.memset(eps[:], EPS).then_inc(s_const, 1)
            pool.wait_ge(s_const, 1)
            pool.affine_select(out=ident[:], in_=ident[:], compare_op=ALU.not_equal, fill=1.0, base=0,
                               pattern=[[-1, P]], channel_multiplier=1).then_inc(s_const, 1)
            pool.wait_ge(s_const, 4)

            def lo(c, n=None):
                pool.wait_ge(s_hi, (c if n is None else n) + 1)
                pool.tensor_tensor(chunk_dst(c, 1), chunk_raw(c), as32(chunk_dst(c, 0)),
                                   ALU.subtract).then_inc(s_lo, 1)

            def ln_rstd(k, h):
                n, cols = 2 * k + h, slice(HALF * h, HALF * (h + 1))
                pool.wait_ge(s_ag, HALF * (n + 1))
                pool.tensor_tensor(veps[:, cols], mv[:, cols, 1], eps[:, 0:HALF], ALU.add).then_inc(s_ve, 1)
                pool.wait_ge(s_ve, n + 1)
                pool.tensor_tensor(rstd[:, cols], veps[:, cols], mhalf[:, 0:HALF], ALU.pow).then_inc(s_rstd, 1)

            def rms_of(par, n, s_in, s_mid, s_done):
                pool.wait_ge(s_in, n)
                pool.tensor_tensor(msq[:, par, :], ssq[:, par, :], eps[:, 0:REP], ALU.add).then_inc(s_mid, 1)
                pool.wait_ge(s_mid, n)
                pool.tensor_tensor(rms[:, par, :], msq[:, par, :], mhalf[:, 0:REP], ALU.pow).then_inc(s_done, 1)

            for k in range(2):
                lo(3 * k)
            ln_rstd(0, 0)
            lo(3 * 2)
            ln_rstd(0, 1)
            lo(3 * 3)
            for c in range(WQ0, WFFN):
                lo(c)
            ln_rstd(1, 0)
            for m in range(2 * T):
                rms_of(m % 2, m + 1, s_ks, s_km, s_kr)
                if m == 1:
                    ln_rstd(1, 1)
                if T + 1 <= m < T + 1 + KT:
                    lo(WFFN + m - (T + 1))
            for c in range(WVAL, WVAL + 2 * KT):
                lo(c)
            for h in range(2):
                ln_rstd(2, h)
            for c in range(WGRP, WGRP + KT):
                lo(c)

            def unit_lo(i, p):
                n, par = unit_at(p, i), i % 2
                pool.wait_ge(s_uha, n + 1)
                pool.tensor_tensor(unit_w(par, 1)[:, 0:2 * D], unit_raw(par, 0)[:, 0:2 * D],
                                   as32(unit_w(par, 0)[:, 0:2 * D]), ALU.subtract).then_inc(s_ula, 1)
                pool.wait_ge(s_uhb, n + 1)
                pool.tensor_tensor(unit_w(par, 1)[:, 2 * D:UW], unit_raw(par, 0)[:, 2 * D:UW],
                                   as32(unit_w(par, 0)[:, 2 * D:UW]), ALU.subtract).then_inc(s_ulb, 1)

            def step(j, p):
                if 0 <= j + 3 and (p is not None or j + 3 < STEPS):
                    i = j + 3
                    rms_of(0, at(p, i) + 1, s_sq, s_ms, s_rr)
                    if j == -1 and p is None:
                        for c in range(WGRP + KT, WGRP + 2 * KT):
                            lo(c)
                    elif j >= 0 and (p is not None or i < STEPS - T):
                        lo(WGRP + T + i, WGRP + T + at(p, i))
                if 0 <= j + 2 and (p is not None or j + 2 < STEPS):
                    i = j + 2
                    pool.wait_ge(s_ri, at(p, i) + 1)
                    pool.tensor_tensor(heads(prob[:]), heads(prob[:]), over(rinv[:, 0:REP], P), ALU.mult)\
                        .then_inc(s_pn, 1)
                if j == -1:
                    for i in range(3):
                        lo(WGRP + T + i)

            for j in range(-3, 0):
                step(j, None)
            with pool.Fori(0, STEPS // BODY - 1) as p:
                for j in range(BODY):
                    step(j, p)
            for j in range(STEPS - BODY, STEPS):
                step(j, None)
                if j == STEPS - 6:
                    unit_lo(0, None)
                if j == STEPS - 4:
                    ln_rstd(3, 0)
            ln_rstd(3, 1)

            unit_lo(1, None)
            with pool.Fori(0, UNITS // 2 - 1) as p:
                for u in range(2):
                    unit_lo(u + 2, p)

        @block.scalar
        def _(act):
            act.dma_start(resid[:, 0:HALF, :], x[0:HALF].rearrange("b p d -> p b d")).then_inc(s_x[0], 16)
            act.dma_start(resid[:, HALF:T, :], x[HALF:T].rearrange("b p d -> p b d")).then_inc(s_x[1], 16)
            act.dma_start(bias[:], bqk).then_inc(s_small, 16)
            act.dma_start(nw[:], norm_w).then_inc(s_small, 16)
            act.dma_start(mask_sb[:], mask).then_inc(s_small, 16)
            act.dma_start(gb[:], gate_b.to_broadcast([P, NR])).then_inc(s_small, 16)

            def hi(c, p=None):
                turn = (c - FIRST) // RING if p is None else (c - FIRST) // RING + p * (BODY // RING)
                if c < FIRST:
                    act.wait_ge(s_first[c], 16)
                else:
                    act.wait_ge(s_raw[c % RING], 16 * (turn + 1))
                act.activation(chunk_dst(c, 0), chunk_raw(c), ACT.Copy).then_inc(s_hi, 1)

            def ln_hi(k, t, keep=False):
                n = T * k + t
                act.wait_ge(s_xt, n + 1)
                src = bank[4 + n % 2][:].rearrange("p (m n) -> p m n", m=KT)
                if keep:
                    act.activation(xnT32[:, :, tile(t)], src, ACT.Copy)
                act.activation(xnT_hi[:, :, tile(t)], src, ACT.Copy).then_inc(s_xhi, 1)

            for c in range(WQ0):
                hi(c)
            act.wait_ge(s_small, 64)
            for n in range(4 * KT):
                m, h = (n % (2 * KT)) // 2, n % 2
                is_q = n // (2 * KT)
                act.wait_ge(s_kq, n + 1)
                dst = (k0T, q0T)[is_q]
                act.activation(dst[:, m, h * D:(h + 1) * D], bank[KQ_BANK[n % 6]][:], ACT.Identity,
                               bias=bias[:, KT * (1 - is_q) + m:KT * (1 - is_q) + m + 1]).then_inc(s_kqe, 1)
                if n < T:
                    ln_hi(0, n)
                if 2 <= n < 2 + KT:
                    hi(WQ0 + n - 2)
                if 2 * KT <= n < 3 * KT:
                    hi(WKEY + n - 2 * KT)
            for c in range(WKEY + KT, WFFN):
                hi(c)
            p0 = norm[:].rearrange("p a n -> p (a n)")
            for b in range(T):
                act.wait_ge(s_nm0, b // HALF + 1)
                act.activation(p0[:, tile(b)], bank[4 + b // HALF][:, tile(b % HALF)], ACT.Exp,
                               bias=nmax[:, b:b + 1], scale=SCALE0, accum_out=rsum[:, b:b + 1]).then_inc(s_ex0, 1)
            for h in range(2):
                act.wait_ge(s_pt0, HALF * (h + 1))
                act.activation((headT, sq)[h][:], bank[6 + h][:], ACT.Copy).then_inc(s_pe0, 1)

            def squares(src, par, s_done):
                for h in range(REP):
                    done = act.activation(sq[:, tile(h)], src[:, tile(h)], ACT.Square, scale=float(P) ** -0.5,
                                          accum_out=ssq[:, par, h:h + 1])
                done.then_inc(s_done, 1)

            act.wait_ge(s_wqk, 1)
            act.wait_ge(s_pv0, T)
            for m in range(2 * T + 2):
                if m < 2 * T:
                    act.wait_ge(s_ka, m + 1)
                    if m >= 2:
                        act.wait_ge(s_kr, m - 1)
                    if m >= 1:
                        act.wait_ge(s_ks, m)
                    squares(bank[6 + m % 2], m % 2, s_ks)
                if 5 <= m < 5 + T:
                    ln_hi(1, m - 5, keep=True)
                if m >= 2:
                    n = m - 2
                    act.wait_ge(s_kt, n + 1)
                    g0 = REP * (n // T)
                    act.activation(keyT.rearrange("p (g n) -> p g n", g=NKV)[:, g0:g0 + REP, tile(n % T)],
                                   heads(bank[2 + n % 2][:]), ACT.Copy, scale=wqk[:, 0:1]).then_inc(s_ke, 1)
                if T + 1 <= m < T + 1 + KT:
                    hi(WFFN + m - (T + 1))
            for c in range(WVAL, WVAL + KT):
                if c == WVAL:
                    act.wait_ge(s_ka, 2 * T)
                hi(c)
            for h in range(2):
                act.wait_ge(s_ht, HALF * (h + 1))
                act.activation(hmT[0:RMAX, h * D:(h + 1) * D], bank[4 + h][0:RMAX, :], ACT.Copy).then_inc(s_he, 1)
            act.wait_ge(s_w, T)
            for c in range(WVAL + KT, WGRP):
                hi(c)
            def copy_values(m):
                act.wait_ge(s_v, m + 1)
                vb, t = divmod(m, T)
                act.activation(val[:, t * NKV * P + vb * D:t * NKV * P + (vb + 1) * D], bank[6 + m % 2][:],
                               ACT.Copy).then_inc(s_ve1, 1)

            for m in range(2 * T - 3):
                copy_values(m)
                if 4 <= m < 4 + T:
                    ln_hi(2, m - 4)
                if T <= m < T + KT:
                    hi(WGRP + m - T)

            def step(j, p):
                def valid(k):
                    return 0 <= k and (p is not None or k < STEPS)
                if valid(j + 1):
                    i = j + 1
                    g = i // T if p is None else 2 * p + i // T
                    if i >= 1 or p is not None:
                        act.wait_ge(s_e, at(p, i))
                    act.activation(vcur_hi[:], val[:, bass.ds(g * P + (i % T) * NKV * P, P)], ACT.Copy)\
                        .then_inc(s_vh, 1)
                if valid(j + 2):
                    act.wait_ge(s_b, at(p, j + 2) + 1)
                    act.activation(headT[:], bank[1][:], ACT.Copy).then_inc(s_qt, 1)
                if valid(j + 3):
                    act.wait_ge(s_a, at(p, j + 3) + 1)
                    squares(bank[0], 0, s_sq)
                if valid(j + 1):
                    act.wait_ge(s_d, at(p, j + 1) + 1)
                    act.activation(probT_hi[:], bank[3][:], ACT.Copy).then_inc(s_pt, 1)
                if valid(j + 2):
                    i = j + 2
                    act.wait_ge(s_mx, at(p, i) + 1)
                    act.wait_ge(s_d, at(p, i))
                    for h in range(REP):
                        done = act.activation(prob[:, tile(h)], score[:, tile(h)], ACT.Exp, bias=nmax[:, h:h + 1],
                                              accum_out=rsum[:, h:h + 1])
                    done.then_inc(s_ex, 1)
                if j == -1:
                    copy_values(2 * T - 1)
                    for c in range(WGRP + KT, WGRP + 2 * KT):
                        hi(c)
                if j >= 0 and (p is not None or j + 3 < STEPS - T):
                    i = j + 3
                    if i % T == KT:
                        act.wait_ge(s_f, at(p, i - KT) + 1)
                    hi(WGRP + T + i, p)
                if valid(j + 1):
                    act.wait_ge(s_e, at(p, j + 1) + 1)
                    act.activation(aoT_hi[:], bank[6][:], ACT.Copy).then_inc(s_ah, 1)
                if j == -1:
                    for i in range(3):
                        hi(WGRP + T + i)

            def unit_hi(i, p, part):
                n, par = unit_at(p, i), i % 2
                act.wait_ge(s_um, n + 1)
                if part == 0:
                    if i >= 2:
                        act.wait_ge(s_g, 2 * (n - 1))
                    act.activation(unit_w(par, 0)[:, 0:2 * D], unit_raw(par, 0)[:, 0:2 * D], ACT.Copy)\
                        .then_inc(s_uha, 1)
                else:
                    if i >= 2:
                        act.wait_ge(s_dn, T * (n - 1))
                    act.activation(unit_w(par, 0)[:, 2 * D:UW], unit_raw(par, 0)[:, 2 * D:UW], ACT.Copy)\
                        .then_inc(s_uhb, 1)

            for j in range(-3, 0):
                step(j, None)
                if j < -1:
                    copy_values(2 * T + j)
            with act.Fori(0, STEPS // BODY - 1) as p:
                for j in range(BODY):
                    step(j, p)
            for j in range(STEPS - BODY, STEPS):
                step(j, None)
                if j == STEPS - 6:
                    unit_hi(0, None, 0)
                    unit_hi(0, None, 1)

            def hidden(i, p):
                n, par = unit_at(p, i), i % 2
                for h in range(2):
                    act.wait_ge(s_g, 2 * n + h + 1)
                    if i >= 1:
                        act.wait_ge(s_hm, 2 * (n - 1) + h + 1)
                    act.activation((score, prob)[h][:], bank[2 * h][:], ACT.Silu).then_inc(s_si, 1)
                    act.wait_ge(s_hm, 2 * n + h + 1)
                    act.activation(unit_h(par, 0)[:, h * D:(h + 1) * D], norm[:, h, :], ACT.Copy).then_inc(s_hh, 1)

            for t in range(T):
                ln_hi(3, t)
            unit_hi(1, None, 0)
            hidden(0, None)
            unit_hi(1, None, 1)
            with act.Fori(0, UNITS // 2 - 1) as p:
                for u in range(2):
                    unit_hi(u + 2, p, 0)
                    hidden(u + 1, p)
                    unit_hi(u + 2, p, 1)
            hidden(UNITS - 1, None)

        @block.vector
        def _(dve):
            def ln_tile_stats(t):
                dve.bn_stats(st[:, t, :], resid[:, t, :]).then_inc(s_st, 1)

            def ln_stats(k, h, done=0):
                for t in range(HALF * h + done, HALF * (h + 1)):
                    ln_tile_stats(t)
                for t in range(HALF * h, HALF * (h + 1)):
                    dve.wait_ge(s_st, T * k + t + 1)
                    dve.bn_aggr(mv[:, t, :], st[:, t, :]).then_inc(s_ag, 1)

            def ln_norm(k, t):
                n = T * k + t
                dve.wait_ge(s_rstd, n // HALF + 1)
                if n >= 2:
                    dve.wait_ge(s_xt, n - 1)
                dve.tensor_scalar(ln_buf[n % 2][:], resid[:, t, :], mv[:, t, 0:1], rstd[:, t:t + 1],
                                  ALU.subtract, ALU.mult).then_inc(s_xn, 1)

            def ln_lo(k, t):
                n = T * k + t
                dve.wait_ge(s_xhi, n + 1)
                dve.tensor_tensor(xnT_lo[:, :, tile(t)], bank[4 + n % 2][:].rearrange("p (m n) -> p m n", m=KT),
                                  as32(xnT_hi[:, :, tile(t)]), ALU.subtract).then_inc(s_xlo, 1)

            def ctx_lo(c):
                dve.wait_ge(s_hi, c + 1)
                dve.tensor_tensor(chunk_dst(c, 1), chunk_raw(c), as32(chunk_dst(c, 0)), ALU.subtract)\
                    .then_inc(s_loc, 1)

            for k in range(KT):
                for h in range(2):
                    ctx_lo(3 * k + 1 + h)
                if k in (1, 2):
                    dve.wait_ge(s_x[k - 1], 16)
                    ln_stats(0, k - 1)
            dve.wait_ge(s_small, 64)
            dve.tensor_tensor(wqk[:], nw[:, 0:1], nw[:, 1:2], ALU.mult).then_inc(s_wqk, 1)
            for t in range(T + 1):
                if t < T:
                    ln_norm(0, t)
                if t >= 1:
                    ln_lo(0, t - 1)
            for h in range(2):
                cols = slice(HALF * h, HALF * (h + 1))
                dve.wait_ge(s_sc0, HALF * (h + 1))
                dve.tensor_reduce(rinv[:, cols], heads(bank[4 + h][:]), AX_X, ALU.max).then_inc(s_mx0, 1)
                dve.wait_ge(s_mx0, h + 1)
                dve.tensor_scalar(nmax[:, cols], rinv[:, cols], -SCALE0, None, ALU.mult).then_inc(s_nm0, 1)
            dve.wait_ge(s_nm0, 2)
            for h in range(2):
                cols = slice(HALF * h, HALF * (h + 1))
                dve.wait_ge(s_ex0, HALF * (h + 1))
                dve.reciprocal(rinv[:, cols], rsum[:, cols]).then_inc(s_ri0, 1)
            for b in range(T):
                dve.wait_ge(s_ri0, b // HALF + 1)
                dve.wait_ge(s_pv0, b + 1)
                dve.scalar_tensor_tensor(out=resid[:, b, :], in0=bank[b % 4][:], scalar=rinv[:, b:b + 1],
                                         in1=resid[:, b, :], op0=ALU.mult, op1=ALU.add).then_inc(s_at0, 1)
                if b % HALF == HALF - 1:
                    dve.wait_ge(s_at0, b + 1)
                    ln_stats(1, b // HALF)
            dve.memset(hmT[RMAX:RMAX + 1, :], 1.0).then_inc(s_one, 1)
            for m in range(2 * T + 1):
                if 3 <= m < 3 + T:
                    ln_norm(1, m - 3)
                if m >= 1:
                    n = m - 1
                    dve.wait_ge(s_kr, n + 1)
                    if n >= 2:
                        dve.wait_ge(s_kt, n - 1)
                    dve.tensor_tensor(heads(norm[:, n % 2, :]), heads(bank[6 + n % 2][:]), over(rms[:, n % 2, :], P),
                                      ALU.mult).then_inc(s_kn, 1)
                if 5 <= m < 5 + T:
                    ln_lo(1, m - 5)
            for h in range(2):
                cols = slice(HALF * h, HALF * (h + 1))
                src = bank[6 + h][:, 0:HALF * (RMAX + NR)].rearrange("p (b n) -> p b n", b=HALF)
                dve.wait_ge(s_h, HALF * (h + 1))
                dve.tensor_copy(hs[:, cols, :], src[:, :, 0:RMAX])
                dve.tensor_tensor(sc[:, cols, :], src[:, :, RMAX:RMAX + NR],
                                  gb[:].unsqueeze(1).to_broadcast([P, HALF, NR]), ALU.add).then_inc(s_rt, 1)
            dve.wait_ge(s_rt, 2)
            dve.tensor_copy(pmax[:, :, 0], sc[:, :, 0]).then_inc(s_rt, 1)
            for r in range(1, NR):
                dve.wait_ge(s_rt, 2 + r)
                dve.tensor_tensor(pmax[:, :, r], pmax[:, :, r - 1], sc[:, :, r], ALU.max).then_inc(s_rt, 1)
            dve.wait_ge(s_rt, 2 + NR)
            dve.tensor_tensor(ind[:], pmax[:, :, 0:NR - 1],
                              pmax[:, :, NR - 1:NR].to_broadcast([P, T, NR - 1]), ALU.is_lt).then_inc(s_rt, 1)
            dve.wait_ge(s_rt, 3 + NR)
            for r in range(1, NR):
                rows = slice(RANKS[r - 1], RANKS[r])
                dve.tensor_tensor(hs[:, :, rows], hs[:, :, rows],
                                  ind[:, :, r - 1:r].to_broadcast([P, T, RANKS[r] - RANKS[r - 1]]), ALU.mult)\
                    .then_inc(s_rt, 1)
            for t in range(T):
                dve.wait_ge(s_w, t + 1)
                dve.tensor_tensor(resid[:, t, :], bank[t % 4][:], resid[:, t, :], ALU.add).then_inc(s_add, 1)
                if t % HALF == HALF - 1:
                    dve.wait_ge(s_add, t + 1)
                    ln_stats(2, t // HALF)
            for t in range(T + 1):
                if t < T:
                    ln_norm(2, t)
                if t >= 1:
                    ln_lo(2, t - 1)

            def step(j, p):
                def valid(k):
                    return 0 <= k and (p is not None or k < STEPS)
                if valid(j + 1):
                    i = j + 1
                    g = i // T if p is None else 2 * p + i // T
                    dve.wait_ge(s_vh, at(p, i) + 1)
                    dve.tensor_tensor(vcur_lo[:], val[:, bass.ds(g * P + (i % T) * NKV * P, P)], as32(vcur_hi[:]),
                                      ALU.subtract).then_inc(s_vl, 1)
                if valid(j + 2):
                    i = j + 2
                    dve.wait_ge(s_c, at(p, i) + 1)
                    dve.wait_ge(s_ex, at(p, i))
                    dve.scalar_tensor_tensor(out=heads(score[:]), in0=heads(bank[2][:]), scalar=SCALE1,
                                             in1=mask_sb[:].unsqueeze(1).to_broadcast([P, REP, P]),
                                             op0=ALU.mult, op1=ALU.add).then_inc(s_sm, 1)
                    dve.wait_ge(s_sm, at(p, i) + 1)
                    dve.tensor_reduce(nmax[:, 0:REP], heads(score[:]), AX_X, ALU.max, negate=True)\
                        .then_inc(s_mx, 1)
                if valid(j + 1):
                    dve.wait_ge(s_pt, at(p, j + 1) + 1)
                    dve.tensor_tensor(probT_lo[:], bank[3][:], as32(probT_hi[:]), ALU.subtract).then_inc(s_ptl, 1)
                if valid(j + 3):
                    i = j + 3
                    dve.wait_ge(s_rr, at(p, i) + 1)
                    dve.tensor_tensor(heads(norm[:, 0, :]), heads(bank[0][:]), over(rms[:, 0, :], P), ALU.mult)\
                        .then_inc(s_qn, 1)
                if valid(j + 2):
                    dve.wait_ge(s_ex, at(p, j + 2) + 1)
                    dve.reciprocal(rinv[:, 0:REP], rsum[:, 0:REP]).then_inc(s_ri, 1)
                if valid(j):
                    dve.wait_ge(s_f, at(p, j) + 1)
                    dve.tensor_tensor(resid[:, j % T, :], bank[7][:], resid[:, j % T, :], ALU.add)\
                        .then_inc(s_add, 1)
                if valid(j + 1):
                    dve.wait_ge(s_ah, at(p, j + 1) + 1)
                    dve.tensor_tensor(aoT_lo[:], bank[6][:], as32(aoT_hi[:]), ALU.subtract).then_inc(s_al, 1)

            for j in range(-3, 0):
                step(j, None)
            with dve.Fori(0, STEPS // BODY - 1) as p:
                for j in range(BODY):
                    step(j, p)
            def dequant(i, p):
                n, par = unit_at(p, i), i % 2
                turn = n // 2 if p is None else p + i // 2
                dve.wait_ge(s_uw[par], 48 * (turn + 1))
                w, z, s = (unit_raw(par, k) for k in range(3))
                dve.tensor_tensor(z, w.bitcast(I32), z.bitcast(I32), ALU.subtract).then_inc(s_us, 1)
                dve.wait_ge(s_us, n + 1)
                dve.tensor_tensor(w, z, s, ALU.mult).then_inc(s_um, 1)

            for j in range(STEPS - BODY, STEPS):
                step(j, None)
                if j == STEPS - 7:
                    dequant(0, None)
                if j == STEPS - HALF - 1:
                    dve.wait_ge(s_add, T + j + 1)
                    ln_stats(3, 0)
                if j == STEPS - 2:
                    dve.wait_ge(s_c, STEPS)
                    dve.wait_ge(s_ex, STEPS)
                    for t in range(HALF + 1):
                        if t < HALF:
                            ln_norm(3, t)
                        if t >= 1:
                            ln_lo(3, t - 1)
                    dve.wait_ge(s_add, T + j + 1)
                    for t in range(HALF, T - 1):
                        ln_tile_stats(t)

            def hidden_up(i, p, h):
                n = unit_at(p, i)
                dve.wait_ge(s_si, 2 * n + h + 1)
                if i >= 1:
                    dve.wait_ge(s_hl, 2 * (n - 1) + h + 1)
                dve.tensor_tensor(norm[:, h, :], (score, prob)[h][:], bank[2 * h + 1][:], ALU.mult)\
                    .then_inc(s_hm, 1)

            def hidden_lo(i, p, h):
                n, par = unit_at(p, i), i % 2
                dve.wait_ge(s_hh, 2 * n + h + 1)
                dve.tensor_tensor(unit_h(par, 1)[:, h * D:(h + 1) * D], norm[:, h, :],
                                  as32(unit_h(par, 0)[:, h * D:(h + 1) * D]), ALU.subtract).then_inc(s_hl, 1)

            def add_down(i, p):
                n = unit_at(p, i)
                for t in range(T):
                    dve.wait_ge(s_dn, T * n + t + 1)
                    dve.tensor_tensor(resid[:, t, :], bank[4 + t % 4][:], resid[:, t, :], ALU.add).then_inc(s_add, 1)

            dve.wait_ge(s_add, T + STEPS)
            ln_stats(3, 1, done=HALF - 1)
            for t in range(HALF, T + 1):
                if t < T:
                    ln_norm(3, t)
                if t > HALF:
                    ln_lo(3, t - 1)
            dequant(1, None)
            for h in range(2):
                hidden_up(0, None, h)
                hidden_lo(0, None, h)
            with dve.Fori(0, UNITS // 2 - 1) as p:
                for u in range(2):
                    dequant(u + 2, p)
                    hidden_up(u + 1, p, 0)
                    hidden_lo(u + 1, p, 0)
                    hidden_up(u + 1, p, 1)
                    add_down(u, p)
                    hidden_lo(u + 1, p, 1)
            for h in range(2):
                hidden_up(UNITS - 1, None, h)
                hidden_lo(UNITS - 1, None, h)
            add_down(UNITS - 2, None)
            add_down(UNITS - 1, None)

        @block.tensor
        def _(pe):
            def three(dst, l_hi, l_lo, r_hi, r_lo, first, last):
                pe.matmul(dst, l_hi, r_hi, start=first, stop=False)
                pe.matmul(dst, l_hi, r_lo, start=False, stop=False)
                return pe.matmul(dst, l_lo, r_hi, start=False, stop=last)

            def ln_transpose(k, t):
                n = T * k + t
                pe.wait_ge(s_xn, n + 1)
                if n >= 2:
                    pe.wait_ge(s_xlo, n - 1)
                for m in range(KT):
                    done = pe.transpose(bank[4 + n % 2][:, tile(m)], ln_buf[n % 2][:, tile(m)], ident[:])
                done.then_inc(s_xt, 1)

            pe.wait_ge(s_const, 4)
            def kq0(n, k):
                m, h = (n % (2 * KT)) // 2, n % 2
                is_q = n // (2 * KT)
                r_hi, r_lo = ((ctxT_hi, ctxT_lo), (xnT_hi, xnT_lo))[is_q]
                done = three(bank[KQ_BANK[n % 6]][:], wbuf(is_q, 0)[:, k, tile(m)], wbuf(is_q, 1)[:, k, tile(m)],
                             r_hi[:, k, h * D:(h + 1) * D], r_lo[:, k, h * D:(h + 1) * D], k == 0, k == KT - 1)
                if k == KT - 1:
                    done.then_inc(s_kq, 1)

            for k in range(KT):
                for c in (3 * k, 3 * k + 2):
                    lo_done(pe, c)
                for n in range(6):
                    kq0(n, k)
                    if k == KT - 1:
                        ln_transpose(0, n)
            for n in range(6, 4 * KT):
                if n == 2 * KT:
                    lo_done(pe, WKEY - 1)
                    pe.wait_ge(s_xlo, T)
                pe.wait_ge(s_kqe, n - 5)
                for k in range(KT):
                    kq0(n, k)
                if n < T:
                    ln_transpose(0, n)
            pe.wait_ge(s_kqe, 4 * KT)
            for b in range(T):
                for m in range(KT):
                    done = pe.matmul(bank[4 + b // HALF][:, tile(b % HALF)], q0T[:, m, tile(b)], k0T[:, m, tile(b)],
                                     start=(m == 0), stop=(m == KT - 1))
                done.then_inc(s_sc0, 1)
            p0 = norm[:].rearrange("p a n -> p (a n)")
            for b in range(T):
                pe.wait_ge(s_ex0, b + 1)
                pe.transpose(bank[6 + b // HALF][:, tile(b % HALF)], p0[:, tile(b)], ident[:]).then_inc(s_pt0, 1)
            pe.wait_ge(s_ctxn, 16)
            for b in range(T):
                pe.wait_ge(s_pe0, b // HALF + 1)
                if b >= 4:
                    pe.wait_ge(s_at0, b - 3)
                pe.matmul(bank[b % 4][:], (headT, sq)[b // HALF][:, tile(b % HALF)], ctxn[:, b, :],
                          start=True, stop=True).then_inc(s_pv0, 1)
            def dense(t):
                for k in range(KT):
                    three(bank[t % 4][:], xnT_hi[:, k, tile(t)], xnT_lo[:, k, tile(t)],
                          wbuf(0, 0)[:, k, :], wbuf(0, 1)[:, k, :], k == 0, False)

            for m in range(2 * T + 2):
                if m < 2 * T:
                    kb, t = divmod(m, T)
                    if t == 0:
                        lo_done(pe, WKEY + KT * (kb + 1) - 1)
                    if m >= 2:
                        pe.wait_ge(s_kn, m - 1)
                    for k in range(KT):
                        done = three(bank[6 + m % 2][:], ctxT_hi[:, k, tile(t)], ctxT_lo[:, k, tile(t)],
                                     wbuf(kb, 0)[:, k, :], wbuf(kb, 1)[:, k, :], k == 0, k == KT - 1)
                    done.then_inc(s_ka, 1)
                else:
                    if m == 2 * T:
                        lo_done(pe, WVAL - 1)
                    dense(m - 2 * T)
                if 4 <= m < 4 + T:
                    ln_transpose(1, m - 4)
                if m >= 2:
                    n = m - 2
                    if n == 0:
                        pe.wait_ge(s_at0, T)
                    pe.wait_ge(s_kn, n + 1)
                    if n >= 2:
                        pe.wait_ge(s_ke, n - 1)
                    for h in range(REP):
                        done = pe.transpose(bank[2 + n % 2][:, tile(h)], norm[:, n % 2, tile(h)], ident[:])
                    done.then_inc(s_kt, 1)
            pe.wait_ge(s_lora, 32)
            pe.wait_ge(s_xlo, 2 * T)
            for t in range(T):
                for k in range(KT):
                    c = (t % HALF) * (RMAX + NR)
                    done = pe.matmul(bank[6 + t // HALF][:, c:c + RMAX + NR], xnT32[:, k, tile(t)], ag_sb[:, k, :],
                                     start=(k == 0), stop=(k == KT - 1))
                done.then_inc(s_h, 1)

            def routed(t):
                pe.matmul(bank[t % 4][:], hmT[:, tile(t)], btb_sb, start=False, stop=True).then_inc(s_w, 1)

            pe.wait_ge(s_ke, 2 * T)
            for t in range(2, HALF):
                dense(t)
            pe.wait_ge(s_rt, 3 + NR + NR - 1)
            for t in range(T):
                pe.transpose(bank[4 + t // HALF][0:RMAX, tile(t % HALF)], hs[:, t, :], ident[:]).then_inc(s_ht, 1)
            pe.wait_ge(s_he, 2)
            pe.wait_ge(s_one, 1)
            for t in range(HALF):
                routed(t)
            for t in range(HALF, T):
                pe.wait_ge(s_add, t - HALF + 1)
                dense(t)
                routed(t)
            def values(m):
                vb, t = divmod(m, T)
                if t == 0:
                    lo_done(pe, WVAL + KT * (vb + 1) - 1)
                if m >= 2:
                    pe.wait_ge(s_ve1, m - 1)
                for k in range(KT):
                    done = three(bank[6 + m % 2][:], ctxT_hi[:, k, tile(t)], ctxT_lo[:, k, tile(t)],
                                 wbuf(1 - vb, 0)[:, k, :], wbuf(1 - vb, 1)[:, k, :], k == 0, k == KT - 1)
                done.then_inc(s_v, 1)

            for m in range(2 * T - 3):
                values(m)
                if 3 <= m < 3 + T:
                    ln_transpose(2, m - 3)
            pe.wait_ge(s_xlo, 3 * T)
            pe.wait_ge(s_add, T)

            def step(j, p):
                def valid(k):
                    return 0 <= k and (p is not None or k < STEPS)
                if valid(j + 2):
                    n = at(p, j + 2)
                    pe.wait_ge(s_qn, n + 1)
                    pe.wait_ge(s_qt, n)
                    for h in range(REP):
                        done = pe.transpose(bank[1][:, tile(h)], norm[:, 0, tile(h)], ident[:])
                    done.then_inc(s_b, 1)
                if valid(j + 3):
                    i = j + 3
                    n, t = at(p, i), i % T
                    if t == 0:
                        lo_done(pe, WGRP + n + KT - 1)
                    pe.wait_ge(s_qn, n)
                    b = WQ_BUF[i // T % 2]
                    for k in range(KT):
                        done = three(bank[0][:], xnT_hi[:, k, tile(t)], xnT_lo[:, k, tile(t)],
                                     wbuf(b, 0)[:, k, :], wbuf(b, 1)[:, k, :], k == 0, k == KT - 1)
                    done.then_inc(s_a, 1)
                if valid(j + 2):
                    i = j + 2
                    n, t = at(p, i), i % T
                    g = i // T if p is None else 2 * p + i // T
                    pe.wait_ge(s_qt, n + 1)
                    pe.wait_ge(s_sm, n)
                    for h in range(REP):
                        done = pe.matmul(bank[2][:, tile(h)], headT[:, tile(h)],
                                         keyT[:, bass.ds(g * TOK + t * P, P)], start=True, stop=True)
                    done.then_inc(s_c, 1)
                if valid(j + 1):
                    n = at(p, j + 1)
                    pe.wait_ge(s_pn, n + 1)
                    pe.wait_ge(s_pt, n)
                    for h in range(REP):
                        done = pe.transpose(bank[3][:, tile(h)], prob[:, tile(h)], ident[:])
                    done.then_inc(s_d, 1)
                if valid(j):
                    n, t = at(p, j), j % T
                    if t == 0:
                        lo_done(pe, WGRP + n + 2 * KT - 1)
                    if j == 0 and p is not None:
                        pe.wait_ge(s_ve1, 2 * T)
                    pe.wait_ge(s_al, n + 1)
                    pe.wait_ge(s_add, T + n)
                    b = WO_BUF[j // T % 2]
                    for h in range(REP):
                        done = three(bank[7][:], aoT_hi[:, tile(h)], aoT_lo[:, tile(h)],
                                     wbuf(b, 0)[:, h, :], wbuf(b, 1)[:, h, :], h == 0, h == REP - 1)
                    done.then_inc(s_f, 1)
                if j == -1:
                    values(2 * T - 1)
                    pe.wait_ge(s_ve1, 2 * T - 1)
                if valid(j + 1):
                    n = at(p, j + 1)
                    pe.wait_ge(s_ptl, n + 1)
                    if j >= 0:
                        pe.wait_ge(s_al, n)
                    three(bank[6][:], vcur_hi[:], vcur_lo[:], probT_hi[:], probT_lo[:], True, True)\
                        .then_inc(s_e, 1)

            for j in range(-3, 0):
                step(j, None)
                if j < -1:
                    values(2 * T + j)
            with pe.Fori(0, STEPS // BODY - 1) as p:
                for j in range(BODY):
                    step(j, p)
            def gate_up(i, p, halves=(0, 1)):
                n, par = unit_at(p, i), i % 2
                pe.wait_ge(s_ula, n + 1)
                for h in halves:
                    if i >= 1:
                        pe.wait_ge(s_hm, 2 * (n - 1) + h + 1)
                    if i == 0:
                        pe.wait_ge(s_xlo, 3 * T + HALF * (h + 1))
                    for u in range(2):
                        for k in range(KT):
                            cols = slice(u * D + k * P, u * D + (k + 1) * P)
                            done = three(bank[2 * h + u][:], unit_w(par, 0)[:, cols], unit_w(par, 1)[:, cols],
                                         xnT_hi[:, k, h * D:(h + 1) * D], xnT_lo[:, k, h * D:(h + 1) * D],
                                         k == 0, k == KT - 1)
                    done.then_inc(s_g, 1)

            def down(i, p):
                n, par = unit_at(p, i), i % 2
                pe.wait_ge(s_ulb, n + 1)
                pe.wait_ge(s_hl, 2 * n + 2)
                for t in range(T):
                    if t >= 4:
                        pe.wait_ge(s_add, DOWN0 + T * n + t - 3)
                    else:
                        pe.wait_ge(s_add, DOWN0 + T * n)
                    three(bank[4 + t % 4][:], unit_h(par, 0)[:, tile(t)], unit_h(par, 1)[:, tile(t)],
                          unit_w(par, 0)[:, 2 * D:UW], unit_w(par, 1)[:, 2 * D:UW], True, True).then_inc(s_dn, 1)

            for j in range(STEPS - BODY, STEPS):
                step(j, None)
                if j == STEPS - 2:
                    for t in range(HALF):
                        ln_transpose(3, t)
            gate_up(0, None, (0,))
            for t in range(HALF, T):
                ln_transpose(3, t)
            gate_up(0, None, (1,))
            with pe.Fori(0, UNITS // 2 - 1) as p:
                for u in range(2):
                    gate_up(u + 1, p)
                    down(u, p)
            gate_up(UNITS - 1, None)
            down(UNITS - 2, None)
            down(UNITS - 1, None)


def _program(nc, shapes):
    args = {n: nc.dram_tensor(f"in_{n}_dram", s, d, kind="ExternalInput").ap() for n, s, d in shapes}
    args["out"] = nc.dram_tensor("out_0_dram", (T, P, D), F32, kind="ExternalOutput").ap()
    cross_attention_ffn(nc, **args)


def kernel(**inputs):
    import numpy as np
    import concourse.bacc as bacc
    from concourse.bass_utils import run_bass_kernel_spmd

    a = {k: np.asarray(v) for k, v in inputs.items()}

    def rows(w):
        return w.T

    def blocks(w, n):
        return w.reshape(-1, P, w.shape[1] // n, n).transpose(2, 0, 1, 3)

    def units(w):
        return w.reshape(KT, P, UNITS, P).transpose(2, 1, 0, 3).reshape(UNITS, P, D)

    def unit_rows(w):
        return w.reshape(KT, UNITS, P).transpose(1, 0, 2).reshape(UNITS, D)

    laid = {
        "x": a["x"],
        "ctx": a["ctx_4096"],
        "ctxT": a["ctx_4096"].reshape(TOK, D).T.reshape(KT, P, TOK),
        "wk0": rows(a["L0_xattn_Wk"]).reshape(KT, P, D),
        "wq0": rows(a["L0_xattn_Wq"]).reshape(KT, P, D),
        "bqk": np.concatenate([a["L0_xattn_bq"].reshape(KT, P).T, a["L0_xattn_bk"].reshape(KT, P).T], 1),
        "wkey": blocks(rows(a["L1_xattn_k_proj_w"]), D).reshape(2 * KT, P, D),
        "wffn": rows(a["L0_ffn_W"]).reshape(KT, P, D),
        "wval": blocks(rows(a["L1_xattn_v_proj_w"]), D).reshape(2 * KT, P, D),
        "agT": rows(np.concatenate([a["L0_ffn_A"], a["L0_ffn_gate_w"]], 0))
            .reshape(KT, P, RMAX + NR).transpose(1, 0, 2),
        "bTb": np.concatenate([rows(a["L0_ffn_B"]), a["L0_ffn_b"][None]], 0),
        "gate_b": a["L0_ffn_gate_b"][None],
        "norm_w": np.stack([a["L1_xattn_q_norm_w"], a["L1_xattn_k_norm_w"]], 1),
        "mask": a["mask_1x1xSxS2_ff0"][0, 0],
        "wqo": np.concatenate([blocks(rows(a["L1_xattn_q_proj_w"]), D),
                               rows(a["L1_xattn_o_proj_w"]).reshape(NKV, REP, P, D)], 1).reshape(-1, P, D),
        "ffn_w": np.concatenate([units(a["L1_ffn_gate_w"]), units(a["L1_ffn_up_w"]),
                                 a["L1_ffn_down_w"].reshape(UNITS, P, D)], 2),
        "ffn_z": np.concatenate([unit_rows(a["L1_ffn_gate_z"]), unit_rows(a["L1_ffn_up_z"]),
                                 a["L1_ffn_down_z"]], 1),
        "ffn_s": np.concatenate([unit_rows(a["L1_ffn_gate_s"]), unit_rows(a["L1_ffn_up_s"]),
                                 a["L1_ffn_down_s"]], 1),
    }
    laid = {k: np.ascontiguousarray(v) for k, v in laid.items()}
    nc = bacc.Bacc("TRN2", target_bir_lowering=False, num_devices=1)
    _program(nc, [(k, v.shape, mybir.dt.from_np(v.dtype)) for k, v in laid.items()])
    r = run_bass_kernel_spmd(nc, [{f"in_{k}_dram": v for k, v in laid.items()}], core_ids=[0])
    return r.results[0]["out_0_dram"]
```

```python
from contextlib import ExitStack

import concourse.bass as bass
from concourse import mybir

F32 = mybir.dt.float32
F32R = mybir.dt.float32r
I32 = mybir.dt.int32
ALU = mybir.AluOpType
ACT = mybir.ActivationFunctionType
AX_X = mybir.AxisListType.X

P = 128
T = 8
HALF = T // 2
D = 512
KT = D // P
TOK = T * P
NKV = 8
REP = 4
RANKS = (8, 16, 32, 64)
RMAX = RANKS[-1]
NR = len(RANKS)
F = 1792
UNITS = F // P
EPS = 1e-5
SCALE0 = 1.0 / float(D) ** 0.5
SCALE1 = 1.0 / float(P) ** 0.5

RING = 4
FIRST = 8
WQ0, WKEY, WFFN, WVAL = 12, 16, 24, 28
WGRP = 36
STEPS = NKV * T
DONE = T + STEPS
BODY = 2 * T


def cross_attention_ffn(nc, x, ctx, ctxT, wk0, wq0, bqk, wkey, wffn, wval, agT, bTb, gate_b, norm_w, mask,
                        wqo, ffn_w, ffn_z, up_s, gd_s, out):
    with ExitStack() as stack:
        def sb(name, shape, dt=F32):
            return stack.enter_context(nc.sbuf_tensor(name, shape, dt))

        def sem(name):
            return stack.enter_context(nc.semaphore(name))

        resid = sb("resid", [P, T, D])
        xnT_hi = sb("xnT_hi", [P, KT, TOK], F32R)
        xnT_lo = sb("xnT_lo", [P, KT, TOK], F32R)
        split = sb("split", [P, 4, 2 * KT * D], F32R)
        kv = sb("kv", [P, 2 * T * KT * 2 * P])
        raw = sb("raw", [P, RING, D])
        sq = sb("sq", [P, D])
        norm = sb("norm", [P, 2, D])
        headT = sb("headT", [P, D])
        score = sb("score", [P, D])
        prob = sb("prob", [P, D])
        probT_hi = sb("probT_hi", [P, D], F32R)
        probT_lo = sb("probT_lo", [P, D], F32R)
        aoT_hi = sb("aoT_hi", [P, D], F32R)
        aoT_lo = sb("aoT_lo", [P, D], F32R)
        vcur_hi = sb("vcur_hi", [P, P], F32R)
        vcur_lo = sb("vcur_lo", [P, P], F32R)
        ident = sb("ident", [P, P])
        mask_sb = sb("mask_sb", [P, P])
        mhalf = sb("mhalf", [P, T])
        eps = sb("eps", [P, T])
        bias = sb("bias", [P, 2 * KT])
        nw = sb("nw", [P, 2])
        wqk = sb("wqk", [P, 1])
        gb = sb("gb", [P, NR])
        gds = sb("gds", [P, UNITS, 2 * KT])
        gate_s = sb("gate_s", [P, 2, KT])
        down_s = sb("down_s", [P, 2, KT])
        st = sb("st", [P, T, 6])
        mv = sb("mv", [P, T, 2])
        veps = sb("veps", [P, T])
        rstd = sb("rstd", [P, T])
        ssq = sb("ssq", [P, 2, REP])
        msq = sb("msq", [P, 2, REP])
        rms = sb("rms", [P, 2, REP])
        nmax = sb("nmax", [P, T])
        rsum = sb("rsum", [P, T])
        rinv = sb("rinv", [P, T])
        sc = sb("sc", [P, T, NR])
        pmax = sb("pmax", [P, T, NR])
        ind = sb("ind", [P, T, NR - 1])

        QUART = KT * TOK
        q0T = kv[:, 0:QUART].rearrange("p (m n) -> p m n", m=KT)
        k0T = kv[:, QUART:2 * QUART].rearrange("p (m n) -> p m n", m=KT)
        ctxn = kv[:, 2 * QUART:3 * QUART].rearrange("p (b n) -> p b n", b=T)
        xnT32 = kv[:, 3 * QUART:4 * QUART].rearrange("p (m n) -> p m n", m=KT)
        o = 2 * QUART
        hs = kv[:, o:o + T * RMAX].rearrange("p (b n) -> p b n", b=T)
        hmT = kv[0:RMAX + 1, o + T * RMAX:o + T * RMAX + TOK]
        o += T * RMAX + TOK
        btb_sb = kv[0:RMAX + 1, o:o + D]
        ag_sb = kv[:, o + D:o + D + KT * (RMAX + NR)].rearrange("p (m n) -> p m n", m=KT)
        keyT = kv[:, 0:2 * QUART]
        val = kv[:, 2 * QUART:4 * QUART]
        UW = 3 * D
        GATE, UP, DOWN = (slice(k * D, (k + 1) * D) for k in range(3))

        def unit_raw(par, which):
            a = par * (2 * UW + D) + which * UW
            return kv[:, a:a + (D if which == 2 else UW)]

        accT = kv[:, 2 * QUART:3 * QUART].rearrange("p (c n) -> p c n", c=KT)

        def unit_w(par, part):
            return split[:, par, part * D:(part + 1) * D]

        def unit_h(par, part):
            a = (2 * par + part) * TOK
            return split[:, 2:4, :].rearrange("p b n -> p (b n)")[:, a:a + TOK]

        def wbuf(b, part):
            return split[:, b, part * KT * D:(part + 1) * KT * D].rearrange("p (m n) -> p m n", m=KT)

        ctxT_hi = split[:, 2, :].rearrange("p (m n) -> p m n", m=KT)
        ctxT_lo = split[:, 3, :].rearrange("p (m n) -> p m n", m=KT)
        KQ_BANK = (0, 1, 2, 3, 6, 7)
        PV_BANK = (2, 3, 4, 5)
        WQ_BUF, WO_BUF = (1, 2), (0, 3)

        def chunk_dst(c, part):
            if c < WQ0:
                k, h = c // 3, c % 3 - 1
                if h < 0:
                    return wbuf(0, part)[:, k, :]
                return (ctxT_hi, ctxT_lo)[part][:, k, h * D:(h + 1) * D]
            if c < WKEY:
                return wbuf(1, part)[:, c - WQ0, :]
            if c < WFFN:
                return wbuf((c - WKEY) // KT, part)[:, c % KT, :]
            if c < WVAL:
                return wbuf(0, part)[:, c - WFFN, :]
            if c < WGRP:
                return wbuf(1 - (c - WVAL) // KT, part)[:, c % KT, :]
            g, k = divmod(c - WGRP, 2 * KT)
            return wbuf((WQ_BUF if k < KT else WO_BUF)[g % 2], part)[:, k % KT, :]

        def chunk_raw(c):
            if c < FIRST:
                return kv[:, 3 * QUART + c * D:3 * QUART + (c + 1) * D]
            return raw[:, c % RING, :]

        p0T = (headT, prob)

        def as32(ap):
            return ap.bitcast(F32)

        def heads(ap):
            return ap.rearrange("p (h n) -> p h n", h=REP)

        def over(col, n):
            return col.unsqueeze(2).to_broadcast([P, col.shape[1], n])

        def tile(t):
            return slice(t * P, (t + 1) * P)

        def ln_buf(k, t):
            return raw[:, t % RING, :] if k == 3 else (headT, score)[t % 2][:]

        def ln_bank(k, t):
            return bank[(4, 5, 0, 1, 4, 5, 7, 0)[t] if k == 3 else 4 + t % 2]

        LN_GROUPS = ((0, HALF), (HALF, T - 1), (T - 1, T))

        bank = [stack.enter_context(nc.psum_tensor(f"bank{i}", [P, D], F32)) for i in range(8)]

        s_first = [sem(f"first_loaded{i}") for i in range(FIRST)]
        s_raw = [sem(f"raw_loaded{i}") for i in range(RING)]
        s_x = [sem("x_loaded0"), sem("x_loaded1")]
        s_ctxn = sem("ctx_loaded")
        s_small = sem("small_loaded")
        s_lora = sem("lora_loaded")
        s_const = sem("const_ready")
        s_wqk = sem("wqk_ready")
        s_hi = sem("chunk_hi")
        s_loc = sem("ctx_chunk_lo")
        s_lo = sem("chunk_lo")
        s_st = sem("ln_stats")
        s_ag = sem("ln_mean_var")
        s_ve = sem("ln_var_eps")
        s_rstd = sem("ln_rstd")
        s_xn = sem("ln_normed")
        s_xt = sem("ln_transposed")
        s_xhi = sem("ln_hi")
        s_xlo = sem("ln_lo")
        s_kq = sem("kq0_product")
        s_kqe = sem("kq0_copied")
        s_sc0 = sem("scores0")
        s_mx0 = sem("max0")
        s_nm0 = sem("negmax0")
        s_ex0 = sem("exp0")
        s_ri0 = sem("rinv0")
        s_pt0 = sem("probs0_transposed")
        s_pe0 = sem("probs0_copied")
        s_pv0 = sem("pv0")
        s_at0 = sem("attended0")
        s_ka = sem("key_product")
        s_ks = sem("key_squares")
        s_km = sem("key_meansq")
        s_kr = sem("key_rms")
        s_kn = sem("key_normed")
        s_kt = sem("key_transposed")
        s_ke = sem("key_copied")
        s_h = sem("lora_down_product")
        s_rt = sem("routing_chain")
        s_ht = sem("lora_transposed")
        s_one = sem("ones_row")
        s_he = sem("lora_copied")
        s_w = sem("ffn0_product")
        s_add = sem("resid_added")
        s_v = sem("value_product")
        s_ve1 = sem("value_copied")
        s_a = sem("q_product")
        s_sq = sem("q_squares")
        s_ms = sem("q_meansq")
        s_rr = sem("q_rms")
        s_qn = sem("q_normed")
        s_b = sem("q_transposed")
        s_qt = sem("q_copied")
        s_c = sem("scores")
        s_sm = sem("masked")
        s_mx = sem("negmax")
        s_ex = sem("exp")
        s_ri = sem("rinv")
        s_pn = sem("probs_normed")
        s_d = sem("probs_transposed")
        s_pt = sem("probs_copied")
        s_ptl = sem("probs_lo")
        s_vh = sem("step_values_hi")
        s_vl = sem("step_values_lo")
        s_e = sem("pv")
        s_ah = sem("attended_hi")
        s_al = sem("attended_lo")
        s_f = sem("out_product")
        s_uw = [sem("unit_loaded0"), sem("unit_loaded1")]
        s_us = sem("unit_up_zero_sub")
        s_um = sem("unit_up_scaled")
        s_uh = sem("unit_up_hi")
        s_ul = sem("unit_up_lo")
        s_ug = sem("unit_gate_ready")
        s_ud = sem("unit_down_ready")
        s_gs = sem("gate_scales")
        s_ds = sem("down_scales")
        s_gp = sem("gate_product")
        s_g0 = sem("gate_scaled")
        s_ga = sem("gate_half_summed")
        s_gc = sem("gate_summed")
        s_u = sem("up_product")
        s_si = sem("silu")
        s_hm = sem("hidden")
        s_hh = sem("hidden_hi")
        s_hl = sem("hidden_lo")
        s_dn = sem("down_product")
        s_acc = sem("down_summed")
        s_hll = sem("last_hidden_lo")
        s_dsc = sem("last_down_scaled")
        s_dga = sem("last_down_summed_by_gpsimd")
        s_ot = sem("sum_transposed")
        s_out = sem("stored")

        block = stack.enter_context(nc.Block())

        def lo_done(eng, c):
            if isinstance(c, int) and c < WQ0 and c % 3:
                eng.wait_ge(s_loc, c - c // 3)
            elif isinstance(c, int) and c < WQ0:
                eng.wait_ge(s_lo, c // 3 + 1)
            else:
                eng.wait_ge(s_lo, c - WQ0 + KT + 1)

        def at(p, k):
            return k if p is None else BODY * p + k

        def unit_at(p, k):
            return k if p is None else 2 * p + k

        POOL_DOWN = ((0, 1), (0, 3), (1, 1))
        gate1 = (headT, sq)

        @block.sync
        def _(sp):
            def load(c, src):
                if c >= FIRST + RING:
                    lo_done(sp, c - RING)
                sp.dma_start(chunk_raw(c), src).then_inc(s_first[c] if c < FIRST else s_raw[c % RING], 16)

            for k in range(KT):
                load(3 * k, wk0[k])
                for h in range(2):
                    load(3 * k + 1 + h, ctxT[k, :, h * D:(h + 1) * D])
                if k in (1, 2):
                    half = slice(HALF * (k - 1), HALF * k)
                    sp.dma_start(resid[:, half, :], x[half].rearrange("b p d -> p b d")).then_inc(s_x[k - 1], 16)
            for dst, src in ((bias, bqk), (nw, norm_w), (mask_sb, mask), (gb, gate_b.to_broadcast([P, NR])),
                             (gds, gd_s)):
                sp.dma_start(dst[:], src).then_inc(s_small, 16)
            for c in range(WQ0, WGRP):
                w, c0 = [(w, c0) for w, c0 in ((wq0, WQ0), (wkey, WKEY), (wffn, WFFN), (wval, WVAL))
                         if c >= c0][-1]
                load(c, w[c - c0])
                if c == WKEY - 1:
                    sp.dma_start(ctxn, ctx.rearrange("b p d -> p b d")).then_inc(s_ctxn, 16)
                if c == WFFN - 1:
                    sp.wait_ge(s_pv0, T)
                    sp.dma_start(ag_sb, agT).then_inc(s_lora, 16)
                    sp.dma_start(btb_sb, bTb).then_inc(s_lora, 16)
            for k in range(2 * KT):
                load(WGRP + k, wqo[k])

            def next_group_chunk(i, p):
                c = WGRP + T + i
                lo_done(sp, WGRP + T + at(p, i) - RING)
                sp.dma_start(raw[:, c % RING, :], wqo[T + i if p is None else BODY * p + (T + i)])\
                    .then_inc(s_raw[c % RING], 16)

            with sp.Fori(0, STEPS // BODY - 1) as p:
                for j in range(BODY):
                    next_group_chunk(j, p)
            for i in range(STEPS - BODY, STEPS - T):
                next_group_chunk(i, None)

            def load_unit(i, par):
                for which, src in ((0, ffn_w[i]), (1, ffn_z[bass.ds(i, 1), :].to_broadcast([P, UW])),
                                   (2, up_s[bass.ds(i, 1), :].to_broadcast([P, D]))):
                    dst = unit_raw(par, which)
                    sp.dma_start(dst if which == 2 else dst.bitcast(I32), src).then_inc(s_uw[par], 16)

            for par in range(2):
                sp.wait_ge(s_c, T * -(-(par + 1) * (2 * UW + D) // TOK))
                load_unit(par, par)
            with sp.Fori(0, UNITS // 2 - 1) as p:
                for u in range(2):
                    sp.wait_ge(s_ud, 2 * p + u + 1)
                    sp.wait_ge(s_ul, 2 * p + u + 1)
                    load_unit(2 * p + u + 2, u)
            for t in range(T):
                sp.wait_ge(s_add, DONE + t + 1)
                sp.dma_start(out[t], resid[:, t, :]).then_inc(s_out, 16)
            sp.wait_ge(s_out, 16 * T)

        @block.gpsimd
        def _(pool):
            pool.memset(ident[:], 0.0).then_inc(s_const, 1)
            pool.memset(mhalf[:], -0.5).then_inc(s_const, 1)
            pool.memset(eps[:], EPS).then_inc(s_const, 1)
            pool.wait_ge(s_const, 1)
            pool.affine_select(out=ident[:], in_=ident[:], compare_op=ALU.not_equal, fill=1.0, base=0,
                               pattern=[[-1, P]], channel_multiplier=1).then_inc(s_const, 1)
            pool.wait_ge(s_const, 4)

            def lo(c, n=None):
                pool.wait_ge(s_hi, (c if n is None else n) + 1)
                pool.tensor_tensor(chunk_dst(c, 1), chunk_raw(c), as32(chunk_dst(c, 0)),
                                   ALU.subtract).then_inc(s_lo, 1)

            def ln_rstd(k, h):
                n = 2 * k + h
                first, end = LN_GROUPS[h] if k == 3 else (HALF * h, HALF * (h + 1))
                cols, size = slice(first, end), end - first
                pool.wait_ge(s_ag, T * k + end)
                pool.tensor_tensor(veps[:, cols], mv[:, cols, 1], eps[:, 0:size], ALU.add).then_inc(s_ve, 1)
                pool.wait_ge(s_ve, n + 1)
                pool.tensor_tensor(rstd[:, cols], veps[:, cols], mhalf[:, 0:size], ALU.pow).then_inc(s_rstd, 1)

            def rms_of(par, n, s_in, s_mid, s_done):
                pool.wait_ge(s_in, n)
                pool.tensor_tensor(msq[:, par, :], ssq[:, par, :], eps[:, 0:REP], ALU.add).then_inc(s_mid, 1)
                pool.wait_ge(s_mid, n)
                pool.tensor_tensor(rms[:, par, :], msq[:, par, :], mhalf[:, 0:REP], ALU.pow).then_inc(s_done, 1)

            for k in range(2):
                lo(3 * k)
            ln_rstd(0, 0)
            lo(3 * 2)
            lo(3 * 3)
            ln_rstd(0, 1)
            for c in range(WQ0, WFFN):
                lo(c)
            for m in range(2 * T):
                rms_of(m % 2, m + 1, s_ks, s_km, s_kr)
                if m in (1, 3):
                    ln_rstd(1, m // 2)
                if T + 1 <= m < T + 1 + KT:
                    lo(WFFN + m - (T + 1))
            for c in range(WVAL, WVAL + 2 * KT):
                lo(c)
            for h in range(2):
                ln_rstd(2, h)
            for c in range(WGRP, WGRP + KT):
                lo(c)

            def up_scale(i, p):
                n, par = unit_at(p, i), i % 2
                pool.wait_ge(s_us, n + 1)
                pool.tensor_tensor(unit_raw(par, 0)[:, UP], unit_raw(par, 1)[:, UP], unit_raw(par, 2), ALU.mult)\
                    .then_inc(s_um, 1)

            def up_lo(i, p):
                n, par = unit_at(p, i), i % 2
                pool.wait_ge(s_uh, n + 1)
                pool.tensor_tensor(unit_w(par, 2), unit_raw(par, 0)[:, UP], as32(unit_w(par, 1)), ALU.subtract)\
                    .then_inc(s_ul, 1)

            def hidden_lo(i, p, h):
                n, par = unit_at(p, i), i % 2
                pool.wait_ge(s_hh, 2 * n + h + 1)
                pool.tensor_tensor(unit_h(par, 1)[:, h * D:(h + 1) * D], norm[:, h, :],
                                   as32(unit_h(par, 0)[:, h * D:(h + 1) * D]), ALU.subtract).then_inc(s_hl, 1)

            def gate_add(i, p, h):
                g = (score, prob)[h]
                pool.wait_ge(s_g0, 2 * (2 * unit_at(p, i) + h) + 2)
                pool.tensor_tensor(g[:], g[:], gate1[h][:], ALU.add).then_inc(s_ga, 1)

            def unit(i, p):
                more = p is not None or i < UNITS - 1
                gate_add(i, p, 0)
                if i >= 1:
                    hidden_lo(i - 1, p, 1)
                if more:
                    up_scale(i + 1, p)
                gate_add(i, p, 1)
                hidden_lo(i, p, 0)
                if more:
                    up_lo(i + 1, p)

            def step(j, p):
                if 0 <= j + 3 and (p is not None or j + 3 < STEPS):
                    i = j + 3
                    rms_of(0, at(p, i) + 1, s_sq, s_ms, s_rr)
                if 0 <= j + 2 and (p is not None or j + 2 < STEPS):
                    i = j + 2
                    pool.wait_ge(s_ri, at(p, i) + 1)
                    pool.tensor_tensor(heads(prob[:]), heads(prob[:]), over(rinv[:, 0:REP], P), ALU.mult)\
                        .then_inc(s_pn, 1)
                if j == -1:
                    for c in range(WGRP + KT, WGRP + 2 * KT):
                        lo(c)
                if j >= 0 and (p is not None or j < STEPS - T):
                    lo(WGRP + T + j, WGRP + T + at(p, j))

            for j in range(-3, 0):
                step(j, None)
            with pool.Fori(0, STEPS // BODY - 1) as p:
                for j in range(BODY):
                    step(j, p)
            for j in range(STEPS - BODY, STEPS):
                step(j, None)
                if j == STEPS - 7:
                    up_scale(0, None)
                if j == STEPS - 5:
                    up_lo(0, None)
                    up_scale(1, None)
                if j == STEPS - 3:
                    up_lo(1, None)
                if j == STEPS - 5:
                    ln_rstd(3, 0)
            ln_rstd(3, 1)
            ln_rstd(3, 2)
            for h in range(2):
                gate_add(0, None, h)
            hidden_lo(0, None, 0)
            unit(1, None)
            with pool.Fori(0, UNITS // 2 - 2) as p:
                for u in range(2):
                    unit(u + 2, p)
            for i in range(UNITS - 2, UNITS):
                unit(i, None)
            for e, (h, c) in enumerate(POOL_DOWN):
                dst = accT[:, c, h * D:(h + 1) * D]
                pool.wait_ge(s_dsc, e + 1)
                pool.wait_ge(s_acc, T * (UNITS - 2) + HALF * h + c + 1)
                pool.tensor_tensor(dst, dst, raw[:, e, :], ALU.add).then_inc(s_dga, 1)

        @block.scalar
        def _(act):
            def hi(c, p=None):
                turn = (c - FIRST) // RING if p is None else (c - FIRST) // RING + p * (BODY // RING)
                if c < FIRST:
                    act.wait_ge(s_first[c], 16)
                else:
                    act.wait_ge(s_raw[c % RING], 16 * (turn + 1))
                act.activation(chunk_dst(c, 0), chunk_raw(c), ACT.Copy).then_inc(s_hi, 1)

            def ln_hi(k, t, keep=False):
                n = T * k + t
                act.wait_ge(s_xt, n + 1)
                src = ln_bank(k, t)[:].rearrange("p (m n) -> p m n", m=KT)
                if keep:
                    act.activation(xnT32[:, :, tile(t)], src, ACT.Copy)
                act.activation(xnT_hi[:, :, tile(t)], src, ACT.Copy).then_inc(s_xhi, 1)

            for c in range(WQ0):
                hi(c)
            for t in range(2):
                ln_hi(0, t)
            hi(WQ0)
            act.wait_ge(s_small, 80)
            for n in range(4 * KT):
                m, h = (n % (2 * KT)) // 2, n % 2
                is_q = n // (2 * KT)
                act.wait_ge(s_kq, n + 1)
                dst = (k0T, q0T)[is_q]
                act.activation(dst[:, m, h * D:(h + 1) * D], bank[KQ_BANK[n % 6]][:], ACT.Identity,
                               bias=bias[:, KT * (1 - is_q) + m:KT * (1 - is_q) + m + 1]).then_inc(s_kqe, 1)
                if n + 2 < T:
                    ln_hi(0, n + 2)
                if 1 <= n < KT:
                    hi(WQ0 + n)
                if 2 * KT <= n < 3 * KT:
                    hi(WKEY + n - 2 * KT)
            for c in range(WKEY + KT, WFFN):
                hi(c)
            p0 = norm[:].rearrange("p a n -> p (a n)")
            for b in range(T):
                act.wait_ge(s_nm0, b // HALF + 1)
                act.activation(p0[:, tile(b)], bank[4 + b // HALF][:, tile(b % HALF)], ACT.Exp,
                               bias=nmax[:, b:b + 1], scale=SCALE0, accum_out=rsum[:, b:b + 1]).then_inc(s_ex0, 1)
            for h in range(2):
                act.wait_ge(s_pt0, HALF * (h + 1))
                act.activation(p0T[h][:], bank[h][:], ACT.Copy).then_inc(s_pe0, 1)

            def squares(src, par, s_done):
                for h in range(REP):
                    done = act.activation(sq[:, tile(h)], src[:, tile(h)], ACT.Square, scale=float(P) ** -0.5,
                                          accum_out=ssq[:, par, h:h + 1])
                done.then_inc(s_done, 1)

            act.wait_ge(s_wqk, 1)
            for m in range(2 * T + 2):
                if m < 2 * T:
                    act.wait_ge(s_ka, m + 1)
                    if m >= 2:
                        act.wait_ge(s_kr, m - 1)
                    if m >= 1:
                        act.wait_ge(s_ks, m)
                    squares(bank[6 + m % 2], m % 2, s_ks)
                if 5 <= m < 5 + T:
                    ln_hi(1, m - 5, keep=True)
                if m >= 2:
                    n = m - 2
                    act.wait_ge(s_kt, n + 1)
                    g0 = REP * (n // T)
                    act.activation(keyT.rearrange("p (g n) -> p g n", g=NKV)[:, g0:g0 + REP, tile(n % T)],
                                   heads(bank[2 + n % 2][:]), ACT.Copy, scale=wqk[:, 0:1]).then_inc(s_ke, 1)
                if T + 1 <= m < T + 1 + KT:
                    hi(WFFN + m - (T + 1))
            for c in range(WVAL, WVAL + KT):
                if c == WVAL:
                    act.wait_ge(s_ka, 2 * T)
                hi(c)
            for h in range(2):
                act.wait_ge(s_ht, HALF * (h + 1))
                act.activation(hmT[0:RMAX, h * D:(h + 1) * D], bank[4 + h][0:RMAX, :], ACT.Copy).then_inc(s_he, 1)
            act.wait_ge(s_w, T)
            for c in range(WVAL + KT, WGRP):
                hi(c)
            def copy_values(m):
                act.wait_ge(s_v, m + 1)
                vb, t = divmod(m, T)
                act.activation(val[:, t * NKV * P + vb * D:t * NKV * P + (vb + 1) * D], bank[6 + m % 2][:],
                               ACT.Copy).then_inc(s_ve1, 1)

            for m in range(2 * T - 3):
                copy_values(m)
                if 4 <= m < 4 + T:
                    ln_hi(2, m - 4)
                if T <= m < T + KT:
                    hi(WGRP + m - T)

            def step(j, p):
                def valid(k):
                    return 0 <= k and (p is not None or k < STEPS)
                if valid(j + 1):
                    i = j + 1
                    g = i // T if p is None else 2 * p + i // T
                    if i >= 1 or p is not None:
                        act.wait_ge(s_e, at(p, i))
                    act.activation(vcur_hi[:], val[:, bass.ds(g * P + (i % T) * NKV * P, P)], ACT.Copy)\
                        .then_inc(s_vh, 1)
                if valid(j + 2):
                    act.wait_ge(s_b, at(p, j + 2) + 1)
                    act.activation(headT[:], bank[1][:], ACT.Copy).then_inc(s_qt, 1)
                if valid(j + 3):
                    act.wait_ge(s_a, at(p, j + 3) + 1)
                    squares(bank[0], 0, s_sq)
                if valid(j + 1):
                    act.wait_ge(s_d, at(p, j + 1) + 1)
                    act.activation(probT_hi[:], bank[3][:], ACT.Copy).then_inc(s_pt, 1)
                if valid(j + 2):
                    i = j + 2
                    act.wait_ge(s_mx, at(p, i) + 1)
                    act.wait_ge(s_d, at(p, i))
                    for h in range(REP):
                        done = act.activation(prob[:, tile(h)], score[:, tile(h)], ACT.Exp, bias=nmax[:, h:h + 1],
                                              accum_out=rsum[:, h:h + 1])
                    done.then_inc(s_ex, 1)
                if j == -1:
                    copy_values(2 * T - 1)
                    for c in range(WGRP + KT, WGRP + 2 * KT):
                        hi(c)
                if j >= 0 and (p is not None or j < STEPS - T):
                    if j % T == KT:
                        act.wait_ge(s_f, at(p, j - KT) + 1)
                    hi(WGRP + T + j, p)
                if p is None and j == STEPS - 2:
                    for t in range(HALF):
                        ln_hi(3, t)
                if valid(j + 1):
                    act.wait_ge(s_e, at(p, j + 1) + 1)
                    act.activation(aoT_hi[:], bank[6][:], ACT.Copy).then_inc(s_ah, 1)

            def up_hi(i, p):
                n, par = unit_at(p, i), i % 2
                act.wait_ge(s_um, n + 1)
                if i >= 2:
                    act.wait_ge(s_u, 2 * (n - 1))
                act.activation(unit_w(par, 1), unit_raw(par, 0)[:, UP], ACT.Copy).then_inc(s_uh, 1)

            for j in range(-3, 0):
                step(j, None)
                if j < -1:
                    copy_values(2 * T + j)
            with act.Fori(0, STEPS // BODY - 1) as p:
                for j in range(BODY):
                    step(j, p)
            for j in range(STEPS - BODY, STEPS):
                step(j, None)
                if j == STEPS - 6:
                    up_hi(0, None)
                if j == STEPS - 4:
                    up_hi(1, None)
                if j == STEPS - 2:
                    act.wait_ge(s_ri, STEPS)
                    act.activation(rsum[:, 0:1], rsum[:, 0:1], ACT.Silu)

            def gate_scale(i, p, h):
                n, par = unit_at(p, i), i % 2
                if h == 0:
                    act.wait_ge(s_gs, n + 1)
                for k in range(2):
                    act.wait_ge(s_gp, KT * (2 * n + h) + k + 1)
                    if i >= 1 and k == 0:
                        act.wait_ge(s_hm, 2 * (n - 1) + h + 1)
                    if i >= 1 and k == 1:
                        act.wait_ge(s_ga, 2 * (n - 1) + h + 1)
                    act.activation((score, prob)[h][:] if k == 0 else gate1[h][:], bank[k][:], ACT.Copy,
                                   scale=gate_s[:, par, k:k + 1]).then_inc(s_g0, 1)

            def silu(i, p, h):
                n = unit_at(p, i)
                act.wait_ge(s_gc, 2 * (2 * n + h + 1))
                act.activation((score, prob)[h][:], (score, prob)[h][:], ACT.Silu).then_inc(s_si, 1)

            def gate_scales(i, p):
                act.activation(gate_s[:, i % 2, :], gds[:, bass.ds(unit_at(p, i), 1), 0:KT], ACT.Copy)\
                    .then_inc(s_gs, 1)

            def down_scales(i, p):
                act.activation(down_s[:, i % 2, :], gds[:, bass.ds(unit_at(p, i), 1), KT:2 * KT], ACT.Copy)\
                    .then_inc(s_ds, 1)

            def hidden_hi(i, p, h):
                n, par = unit_at(p, i), i % 2
                act.wait_ge(s_hm, 2 * n + h + 1)
                if i >= 2:
                    act.wait_ge(s_dn, T * (n - 2) + HALF * (h + 1))
                act.activation(unit_h(par, 0)[:, h * D:(h + 1) * D], norm[:, h, :], ACT.Copy).then_inc(s_hh, 1)

            def unit(i, p):
                gate_scale(i, p, 0)
                if i >= 1:
                    hidden_hi(i - 1, p, 1)
                silu(i, p, 0)
                down_scales(i, p)
                if p is not None or i < UNITS - 1:
                    gate_scales(i + 1, p)
                gate_scale(i, p, 1)
                hidden_hi(i, p, 0)
                if p is not None or i < UNITS - 1:
                    up_hi(i + 1, p)
                silu(i, p, 1)

            gate_scales(0, None)
            gate_scale(0, None, 0)
            for t in range(HALF, T):
                ln_hi(3, t)
            silu(0, None, 0)
            down_scales(0, None)
            gate_scales(1, None)
            gate_scale(0, None, 1)
            hidden_hi(0, None, 0)
            silu(0, None, 1)
            unit(1, None)
            with act.Fori(0, UNITS // 2 - 2) as p:
                for u in range(2):
                    unit(u + 2, p)
            for i in range(UNITS - 2, UNITS):
                unit(i, None)
            hidden_hi(UNITS - 1, None, 1)
            for e, (h, c) in enumerate(POOL_DOWN):
                act.wait_ge(s_dn, T * (UNITS - 1) + HALF * h + c + 1)
                act.activation(raw[:, e, :], bank[4 + c][:], ACT.Copy,
                               scale=down_s[:, (UNITS - 1) % 2, c:c + 1]).then_inc(s_dsc, 1)

        @block.vector
        def _(dve):
            def ln_tile_stats(t):
                dve.bn_stats(st[:, t, :], resid[:, t, :]).then_inc(s_st, 1)

            def ln_stats(k, h, first=None, end=None, done=0):
                first, end = HALF * h if first is None else first, HALF * (h + 1) if end is None else end
                for t in range(first + done, end):
                    ln_tile_stats(t)
                for t in range(first, end):
                    dve.wait_ge(s_st, T * k + t + 1)
                    dve.bn_aggr(mv[:, t, :], st[:, t, :]).then_inc(s_ag, 1)

            def ln_norm(k, t):
                n = T * k + t
                group = [h for h, (first, _) in enumerate(LN_GROUPS) if t >= first][-1] if k == 3 else t // HALF
                dve.wait_ge(s_rstd, 2 * k + group + 1)
                ring = RING if k == 3 else 2
                if n >= ring and not (k == 3 and t < ring):
                    dve.wait_ge(s_xt, n - ring + 1)
                dve.tensor_scalar(ln_buf(k, t), resid[:, t, :], mv[:, t, 0:1], rstd[:, t:t + 1],
                                  ALU.subtract, ALU.mult).then_inc(s_xn, 1)

            def ln_lo(k, t):
                n = T * k + t
                dve.wait_ge(s_xhi, n + 1)
                dve.tensor_tensor(xnT_lo[:, :, tile(t)], ln_bank(k, t)[:].rearrange("p (m n) -> p m n", m=KT),
                                  as32(xnT_hi[:, :, tile(t)]), ALU.subtract).then_inc(s_xlo, 1)

            def ctx_lo(c):
                dve.wait_ge(s_hi, c + 1)
                dve.tensor_tensor(chunk_dst(c, 1), chunk_raw(c), as32(chunk_dst(c, 0)), ALU.subtract)\
                    .then_inc(s_loc, 1)

            for k in range(KT):
                for h in range(2):
                    ctx_lo(3 * k + 1 + h)
                if k in (1, 2):
                    if k == 2:
                        ln_norm(0, 0)
                        ln_norm(0, 1)
                    dve.wait_ge(s_x[k - 1], 16)
                    ln_stats(0, k - 1)
            dve.wait_ge(s_small, 80)
            dve.tensor_tensor(wqk[:], nw[:, 0:1], nw[:, 1:2], ALU.mult).then_inc(s_wqk, 1)
            for t in range(T):
                ln_lo(0, t)
                if t + 2 < T:
                    ln_norm(0, t + 2)
            for h in range(2):
                cols = slice(HALF * h, HALF * (h + 1))
                dve.wait_ge(s_sc0, HALF * (h + 1))
                dve.tensor_reduce(rinv[:, cols], heads(bank[4 + h][:]), AX_X, ALU.max).then_inc(s_mx0, 1)
                dve.wait_ge(s_mx0, h + 1)
                dve.tensor_scalar(nmax[:, cols], rinv[:, cols], -SCALE0, None, ALU.mult).then_inc(s_nm0, 1)
            dve.wait_ge(s_nm0, 2)
            for h in range(2):
                cols = slice(HALF * h, HALF * (h + 1))
                dve.wait_ge(s_ex0, HALF * (h + 1))
                dve.reciprocal(rinv[:, cols], rsum[:, cols]).then_inc(s_ri0, 1)
            def key_norm(n):
                dve.wait_ge(s_kr, n + 1)
                if n == 0:
                    dve.wait_ge(s_pt0, T)
                if n >= 2:
                    dve.wait_ge(s_kt, n - 1)
                dve.tensor_tensor(heads(norm[:, n % 2, :]), heads(bank[6 + n % 2][:]), over(rms[:, n % 2, :], P),
                                  ALU.mult).then_inc(s_kn, 1)

            for b in range(T):
                if b % HALF == 0:
                    key_norm(b // HALF)
                dve.wait_ge(s_ri0, b // HALF + 1)
                dve.wait_ge(s_pv0, b + 1)
                dve.scalar_tensor_tensor(out=resid[:, b, :], in0=bank[PV_BANK[b % 4]][:], scalar=rinv[:, b:b + 1],
                                         in1=resid[:, b, :], op0=ALU.mult, op1=ALU.add).then_inc(s_at0, 1)
            for m in range(2, 2 * T + 1):
                if m == 2:
                    dve.wait_ge(s_at0, T)
                    ln_stats(1, 0)
                if 3 <= m < 3 + T:
                    ln_norm(1, m - 3)
                if m >= 3:
                    key_norm(m - 1)
                if m == 3:
                    ln_tile_stats(HALF)
                    ln_tile_stats(HALF + 1)
                if m == 4:
                    ln_stats(1, 1, done=2)
                if m == 6:
                    dve.memset(hmT[RMAX:RMAX + 1, :], 1.0).then_inc(s_one, 1)
                if 5 <= m < 5 + T:
                    ln_lo(1, m - 5)
            for h in range(2):
                cols = slice(HALF * h, HALF * (h + 1))
                src = bank[6 + h][:, 0:HALF * (RMAX + NR)].rearrange("p (b n) -> p b n", b=HALF)
                dve.wait_ge(s_h, HALF * (h + 1))
                dve.tensor_copy(hs[:, cols, :], src[:, :, 0:RMAX])
                dve.tensor_tensor(sc[:, cols, :], src[:, :, RMAX:RMAX + NR],
                                  gb[:].unsqueeze(1).to_broadcast([P, HALF, NR]), ALU.add).then_inc(s_rt, 1)
            dve.wait_ge(s_rt, 2)
            dve.tensor_copy(pmax[:, :, 0], sc[:, :, 0]).then_inc(s_rt, 1)
            for r in range(1, NR):
                dve.wait_ge(s_rt, 2 + r)
                dve.tensor_tensor(pmax[:, :, r], pmax[:, :, r - 1], sc[:, :, r], ALU.max).then_inc(s_rt, 1)
            dve.wait_ge(s_rt, 2 + NR)
            dve.tensor_tensor(ind[:], pmax[:, :, 0:NR - 1],
                              pmax[:, :, NR - 1:NR].to_broadcast([P, T, NR - 1]), ALU.is_lt).then_inc(s_rt, 1)
            dve.wait_ge(s_rt, 3 + NR)
            for r in range(1, NR):
                rows = slice(RANKS[r - 1], RANKS[r])
                dve.tensor_tensor(hs[:, :, rows], hs[:, :, rows],
                                  ind[:, :, r - 1:r].to_broadcast([P, T, RANKS[r] - RANKS[r - 1]]), ALU.mult)\
                    .then_inc(s_rt, 1)
            for t in range(T):
                dve.wait_ge(s_w, t + 1)
                dve.tensor_tensor(resid[:, t, :], bank[t % 4][:], resid[:, t, :], ALU.add).then_inc(s_add, 1)
                if t % HALF == HALF - 1:
                    dve.wait_ge(s_add, t + 1)
                    ln_stats(2, t // HALF)
            for t in range(T + 1):
                if t < T:
                    ln_norm(2, t)
                if t >= 1:
                    ln_lo(2, t - 1)

            def add_out(j, p):
                dve.wait_ge(s_f, at(p, j) + 1)
                dve.tensor_tensor(resid[:, j % T, :], bank[7][:], resid[:, j % T, :], ALU.add).then_inc(s_add, 1)

            def step(j, p):
                def valid(k):
                    return 0 <= k and (p is not None or k < STEPS)
                if valid(j + 1):
                    i = j + 1
                    g = i // T if p is None else 2 * p + i // T
                    dve.wait_ge(s_vh, at(p, i) + 1)
                    dve.tensor_tensor(vcur_lo[:], val[:, bass.ds(g * P + (i % T) * NKV * P, P)], as32(vcur_hi[:]),
                                      ALU.subtract).then_inc(s_vl, 1)
                if valid(j + 2):
                    i = j + 2
                    dve.wait_ge(s_c, at(p, i) + 1)
                    dve.wait_ge(s_ex, at(p, i))
                    dve.scalar_tensor_tensor(out=heads(score[:]), in0=heads(bank[2][:]), scalar=SCALE1,
                                             in1=mask_sb[:].unsqueeze(1).to_broadcast([P, REP, P]),
                                             op0=ALU.mult, op1=ALU.add).then_inc(s_sm, 1)
                    dve.wait_ge(s_sm, at(p, i) + 1)
                    dve.tensor_reduce(nmax[:, 0:REP], heads(score[:]), AX_X, ALU.max, negate=True)\
                        .then_inc(s_mx, 1)
                if valid(j + 1):
                    dve.wait_ge(s_pt, at(p, j + 1) + 1)
                    dve.tensor_tensor(probT_lo[:], bank[3][:], as32(probT_hi[:]), ALU.subtract).then_inc(s_ptl, 1)
                if valid(j + 3):
                    i = j + 3
                    dve.wait_ge(s_rr, at(p, i) + 1)
                    dve.tensor_tensor(heads(norm[:, 0, :]), heads(bank[0][:]), over(rms[:, 0, :], P), ALU.mult)\
                        .then_inc(s_qn, 1)
                if valid(j + 2):
                    dve.wait_ge(s_ex, at(p, j + 2) + 1)
                    dve.reciprocal(rinv[:, 0:REP], rsum[:, 0:REP]).then_inc(s_ri, 1)
                if p is None and j == STEPS - 4:
                    lo_done(dve, WGRP + STEPS - 1)
                    for t in range(HALF):
                        ln_norm(3, t)
                if p is None and j == STEPS - 2:
                    for t in range(HALF):
                        ln_lo(3, t)
                if p is None and j == STEPS - 3:
                    dve.wait_ge(s_add, T + STEPS - 3)
                    ln_tile_stats(HALF)
                if valid(j) and (p is not None or j < STEPS - 1):
                    add_out(j, p)
                if valid(j + 1):
                    dve.wait_ge(s_ah, at(p, j + 1) + 1)
                    dve.tensor_tensor(aoT_lo[:], bank[6][:], as32(aoT_hi[:]), ALU.subtract).then_inc(s_al, 1)

            for j in range(-3, 0):
                step(j, None)
            with dve.Fori(0, STEPS // BODY - 1) as p:
                for j in range(BODY):
                    step(j, p)
            def sub_up(i, p):
                n, par = unit_at(p, i), i % 2
                turn = n // 2 if p is None else p + i // 2
                dve.wait_ge(s_uw[par], 48 * (turn + 1))
                zero = unit_raw(par, 1)[:, UP]
                dve.tensor_tensor(zero, unit_raw(par, 0)[:, UP].bitcast(I32), zero.bitcast(I32), ALU.subtract)\
                    .then_inc(s_us, 1)

            def sub(par, cols, part, done):
                dve.tensor_tensor(unit_w(par, part), unit_raw(par, 0)[:, cols].bitcast(I32),
                                  unit_raw(par, 1)[:, cols].bitcast(I32), ALU.subtract).then_inc(done, 1)

            def sub_gate(i, p):
                if i >= 2:
                    dve.wait_ge(s_gp, 2 * KT * (unit_at(p, i) - 1))
                sub(i % 2, GATE, 0, s_ug)

            def sub_down(i, p):
                if i >= 2:
                    dve.wait_ge(s_dn, T * (unit_at(p, i) - 1))
                sub(i % 2, DOWN, 3, s_ud)

            for j in range(STEPS - BODY, STEPS):
                step(j, None)
                if j == STEPS - 8:
                    sub_up(0, None)
                if j == STEPS - 7:
                    sub_gate(0, None)
                    sub_down(0, None)
                if j == STEPS - 6:
                    sub_up(1, None)
                    sub_gate(1, None)
                if j == STEPS - HALF - 1:
                    dve.wait_ge(s_add, T + j + 1)
                    ln_stats(3, 0)

            def gate_sum(i, p, h, k):
                n, par = unit_at(p, i), i % 2
                g = (score, prob)[h]
                dve.wait_ge(s_gp, KT * (2 * n + h) + k + 1)
                if k == 2:
                    dve.wait_ge(s_ga, 2 * n + h + 1)
                else:
                    dve.wait_ge(s_gc, 2 * (2 * n + h) + 1)
                dve.scalar_tensor_tensor(out=g[:], in0=bank[k][:], scalar=gate_s[:, par, k:k + 1], in1=g[:],
                                         op0=ALU.mult, op1=ALU.add).then_inc(s_gc, 1)

            def hidden_up(i, p, h):
                n = unit_at(p, i)
                dve.wait_ge(s_si, 2 * n + h + 1)
                dve.wait_ge(s_u, 2 * n + h + 1)
                if i >= 1:
                    dve.wait_ge(s_hl, 2 * (n - 1) + h + 1)
                dve.tensor_tensor(norm[:, h, :], (score, prob)[h][:], bank[6 + h][:], ALU.mult).then_inc(s_hm, 1)

            def add_down(i, p, h, c):
                if i < 0:
                    return
                n, dst, scale = unit_at(p, i), accT[:, c, h * D:(h + 1) * D], down_s[:, i % 2, c:c + 1]
                src = bank[4 + (c if p is None and i == UNITS - 1 else c % 2)][:]
                if h == 0 and c == 0:
                    dve.wait_ge(s_ds, n + 1)
                dve.wait_ge(s_dn, T * n + HALF * h + c + 1)
                if i == 0 and p is None:
                    dve.tensor_scalar(dst, src, scale, None, ALU.mult).then_inc(s_acc, 1)
                else:
                    dve.scalar_tensor_tensor(out=dst, in0=src, scalar=scale, in1=dst,
                                             op0=ALU.mult, op1=ALU.add).then_inc(s_acc, 1)

            def unit(i, p):
                sub_down(i, p)
                more = p is not None or i < UNITS - 1
                starting = p is None and i == 1
                for h in range(2):
                    add_down(i - 1, p, h, 0)
                    if starting and h == 0:
                        add_down(i - 1, p, h, 1)
                    gate_sum(i, p, h, 2)
                    gate_sum(i, p, h, 3)
                    if not (starting and h == 0):
                        add_down(i - 1, p, h, 1)
                    if h == 0 and more:
                        sub_up(i + 1, p)
                    hidden_up(i, p, h)
                    add_down(i - 1, p, h, 2)
                    add_down(i - 1, p, h, 3)
                    if h == 0 and more:
                        sub_gate(i + 1, p)

            dve.wait_ge(s_add, T + STEPS - 1)
            ln_stats(3, 1, end=T - 1, done=1)
            for t in range(HALF, T - 1):
                ln_norm(3, t)
            add_out(STEPS - 1, None)
            dve.wait_ge(s_add, T + STEPS)
            ln_stats(3, 1, first=T - 1)
            ln_lo(3, HALF)
            ln_lo(3, HALF + 1)
            ln_norm(3, T - 1)
            for t in range(HALF + 2, T):
                ln_lo(3, t)
            gate_sum(0, None, 0, 2)
            gate_sum(0, None, 0, 3)
            hidden_up(0, None, 0)
            for k in range(2, KT):
                gate_sum(0, None, 1, k)
            hidden_up(0, None, 1)
            unit(1, None)
            with dve.Fori(0, UNITS // 2 - 2) as p:
                for u in range(2):
                    unit(u + 2, p)
            for i in range(UNITS - 2, UNITS):
                unit(i, None)
            dve.wait_ge(s_hh, 2 * UNITS)
            last = (UNITS - 1) % 2
            dve.tensor_tensor(unit_h(last, 1)[:, D:2 * D], norm[:, 1, :], as32(unit_h(last, 0)[:, D:2 * D]),
                              ALU.subtract).then_inc(s_hll, 1)
            for h in range(2):
                for c in range(KT):
                    if (h, c) not in POOL_DOWN:
                        add_down(UNITS - 1, None, h, c)
            for t in range(T):
                dve.wait_ge(s_ot, t + 1)
                dve.tensor_tensor(resid[:, t, :], bank[t % 4][:], resid[:, t, :], ALU.add).then_inc(s_add, 1)

        @block.tensor
        def _(pe):
            def three(dst, l_hi, l_lo, r_hi, r_lo, first, last):
                pe.matmul(dst, l_hi, r_hi, start=first, stop=False)
                pe.matmul(dst, l_hi, r_lo, start=False, stop=False)
                return pe.matmul(dst, l_lo, r_hi, start=False, stop=last)

            def ln_transpose(k, t):
                n = T * k + t
                pe.wait_ge(s_xn, n + 1)
                if k == 3 and t == T - 2:
                    pe.wait_ge(s_add, T + STEPS)
                elif k == 3 and t == T - 1:
                    pe.wait_ge(s_g0, 1)
                elif k == 3 and t >= HALF:
                    pe.wait_ge(s_xlo, n - 3)
                elif n >= 2 and not (k == 3 and t < HALF):
                    pe.wait_ge(s_xlo, n - 1)
                for m in range(KT):
                    done = pe.transpose(ln_bank(k, t)[:, tile(m)], ln_buf(k, t)[:, tile(m)], ident[:])
                done.then_inc(s_xt, 1)

            pe.wait_ge(s_const, 4)
            def kq0(n, k):
                m, h = (n % (2 * KT)) // 2, n % 2
                is_q = n // (2 * KT)
                r_hi, r_lo = ((ctxT_hi, ctxT_lo), (xnT_hi, xnT_lo))[is_q]
                done = three(bank[KQ_BANK[n % 6]][:], wbuf(is_q, 0)[:, k, tile(m)], wbuf(is_q, 1)[:, k, tile(m)],
                             r_hi[:, k, h * D:(h + 1) * D], r_lo[:, k, h * D:(h + 1) * D], k == 0, k == KT - 1)
                if k == KT - 1:
                    done.then_inc(s_kq, 1)

            for k in range(KT):
                lo_done(pe, 3 * k)
                lo_done(pe, 3 * k + 1)
                for n in (0, 2, 4, 1, 3, 5) if k == 0 else range(6):
                    if n == 1:
                        lo_done(pe, 3 * k + 2)
                    kq0(n, k)
                    if k == KT - 2 and n in (3, 5):
                        ln_transpose(0, n // 4)
                    if k == KT - 1:
                        ln_transpose(0, n + 2)
            for n in range(6, 4 * KT):
                if n == 2 * KT:
                    lo_done(pe, WKEY - 1)
                    pe.wait_ge(s_xlo, T)
                pe.wait_ge(s_kqe, n - 5)
                for k in range(KT):
                    kq0(n, k)
            for b in range(T):
                if b % HALF == 0:
                    pe.wait_ge(s_kqe, 4 * KT - 1 + b // HALF)
                for m in range(KT):
                    done = pe.matmul(bank[4 + b // HALF][:, tile(b % HALF)], q0T[:, m, tile(b)], k0T[:, m, tile(b)],
                                     start=(m == 0), stop=(m == KT - 1))
                done.then_inc(s_sc0, 1)
            def keys(m):
                kb, t = divmod(m, T)
                if t == 0:
                    lo_done(pe, WKEY + KT * (kb + 1) - 1)
                if m >= 2:
                    pe.wait_ge(s_kn, m - 1)
                for k in range(KT):
                    done = three(bank[6 + m % 2][:], ctxT_hi[:, k, tile(t)], ctxT_lo[:, k, tile(t)],
                                 wbuf(kb, 0)[:, k, :], wbuf(kb, 1)[:, k, :], k == 0, k == KT - 1)
                done.then_inc(s_ka, 1)

            keys(0)
            p0 = norm[:].rearrange("p a n -> p (a n)")
            for b in range(T):
                pe.wait_ge(s_ex0, b + 1)
                pe.transpose(bank[b // HALF][:, tile(b % HALF)], p0[:, tile(b)], ident[:]).then_inc(s_pt0, 1)
            keys(1)
            pe.wait_ge(s_ctxn, 16)
            for b in range(T):
                pe.wait_ge(s_pe0, b // HALF + 1)
                if b >= 4:
                    pe.wait_ge(s_at0, b - 3)
                pe.matmul(bank[PV_BANK[b % 4]][:], p0T[b // HALF][:, tile(b % HALF)], ctxn[:, b, :],
                          start=True, stop=True).then_inc(s_pv0, 1)
            def dense(t):
                for k in range(KT):
                    three(bank[t % 4][:], xnT_hi[:, k, tile(t)], xnT_lo[:, k, tile(t)],
                          wbuf(0, 0)[:, k, :], wbuf(0, 1)[:, k, :], k == 0, False)

            for m in range(2, 2 * T + 2):
                if m < 2 * T:
                    keys(m)
                else:
                    if m == 2 * T:
                        lo_done(pe, WVAL - 1)
                    dense(m - 2 * T)
                if 4 <= m < 4 + T:
                    ln_transpose(1, m - 4)
                if m >= 2:
                    n = m - 2
                    if n == 0:
                        pe.wait_ge(s_at0, T)
                    pe.wait_ge(s_kn, n + 1)
                    if n >= 2:
                        pe.wait_ge(s_ke, n - 1)
                    for h in range(REP):
                        done = pe.transpose(bank[2 + n % 2][:, tile(h)], norm[:, n % 2, tile(h)], ident[:])
                    done.then_inc(s_kt, 1)
            pe.wait_ge(s_lora, 32)
            pe.wait_ge(s_xlo, 2 * T)
            for t in range(T):
                for k in range(KT):
                    c = (t % HALF) * (RMAX + NR)
                    done = pe.matmul(bank[6 + t // HALF][:, c:c + RMAX + NR], xnT32[:, k, tile(t)], ag_sb[:, k, :],
                                     start=(k == 0), stop=(k == KT - 1))
                done.then_inc(s_h, 1)

            def routed(t):
                pe.matmul(bank[t % 4][:], hmT[:, tile(t)], btb_sb, start=False, stop=True).then_inc(s_w, 1)

            pe.wait_ge(s_ke, 2 * T)
            for t in range(2, HALF):
                dense(t)
            pe.wait_ge(s_rt, 3 + NR + NR - 1)
            for t in range(T):
                pe.transpose(bank[4 + t // HALF][0:RMAX, tile(t % HALF)], hs[:, t, :], ident[:]).then_inc(s_ht, 1)
            pe.wait_ge(s_he, 1)
            pe.wait_ge(s_one, 1)
            for t in range(HALF):
                routed(t)
            pe.wait_ge(s_he, 2)
            for t in range(HALF, T):
                pe.wait_ge(s_add, t - HALF + 1)
                dense(t)
                routed(t)
            def values(m):
                vb, t = divmod(m, T)
                if t == 0:
                    lo_done(pe, WVAL + KT * (vb + 1) - 1)
                if m >= 2:
                    pe.wait_ge(s_ve1, m - 1)
                for k in range(KT):
                    done = three(bank[6 + m % 2][:], ctxT_hi[:, k, tile(t)], ctxT_lo[:, k, tile(t)],
                                 wbuf(1 - vb, 0)[:, k, :], wbuf(1 - vb, 1)[:, k, :], k == 0, k == KT - 1)
                done.then_inc(s_v, 1)

            for m in range(2 * T - 3):
                values(m)
                if 3 <= m < 3 + T:
                    ln_transpose(2, m - 3)
            pe.wait_ge(s_xlo, 3 * T)
            pe.wait_ge(s_add, T)

            def gate(i, p, h):
                n, par = unit_at(p, i), i % 2
                if h == 0:
                    pe.wait_ge(s_ug, n + 1)
                if i == 0:
                    pe.wait_ge(s_xlo, 3 * T + HALF * (h + 1))
                for k in range(KT):
                    if i >= 1 or h == 1:
                        if k < 2:
                            pe.wait_ge(s_g0, 2 * (2 * n + h - 1) + k + 1)
                        else:
                            pe.wait_ge(s_gc, 2 * (2 * n + h - 1) + k - 1)
                    w = unit_w(par, 0)[:, tile(k)]
                    pe.matmul(bank[k][:], w, xnT_hi[:, k, h * D:(h + 1) * D], start=True, stop=False)
                    pe.matmul(bank[k][:], w, xnT_lo[:, k, h * D:(h + 1) * D], start=False, stop=True)\
                        .then_inc(s_gp, 1)

            def up(i, p, h, tiles=range(KT)):
                n, par = unit_at(p, i), i % 2
                if h == 0 and 0 in tiles:
                    pe.wait_ge(s_ul, n + 1)
                if i >= 1:
                    pe.wait_ge(s_hm, 2 * (n - 1) + h + 1)
                for k in tiles:
                    done = three(bank[6 + h][:], unit_w(par, 1)[:, tile(k)], unit_w(par, 2)[:, tile(k)],
                                 xnT_hi[:, k, h * D:(h + 1) * D], xnT_lo[:, k, h * D:(h + 1) * D],
                                 k == 0, k == KT - 1)
                if KT - 1 in tiles:
                    done.then_inc(s_u, 1)

            def down(i, p, h, columns):
                if i < 0:
                    return
                n, par = unit_at(p, i), i % 2
                for c in columns:
                    if c == 0:
                        if h == 0:
                            pe.wait_ge(s_ud, n + 1)
                        pe.wait_ge(s_hl, 2 * n + h + 1)
                    if i >= 1 or 2 * h + c >= 2:
                        pe.wait_ge(s_acc, T * n + HALF * h + c - 1)
                    w = unit_w(par, 3)[:, tile(c)]
                    pe.matmul(bank[4 + c % 2][:], w, unit_h(par, 0)[:, h * D:(h + 1) * D], start=True, stop=False)
                    pe.matmul(bank[4 + c % 2][:], w, unit_h(par, 1)[:, h * D:(h + 1) * D], start=False, stop=True)\
                        .then_inc(s_dn, 1)

            def step(j, p):
                def valid(k):
                    return 0 <= k and (p is not None or k < STEPS)
                if valid(j + 2):
                    n = at(p, j + 2)
                    pe.wait_ge(s_qn, n + 1)
                    pe.wait_ge(s_qt, n)
                    for h in range(REP):
                        done = pe.transpose(bank[1][:, tile(h)], norm[:, 0, tile(h)], ident[:])
                    done.then_inc(s_b, 1)
                if p is None and j == STEPS - 3:
                    for t in range(2):
                        ln_transpose(3, t)
                if p is None and j == STEPS - 2:
                    for t in range(2, HALF):
                        ln_transpose(3, t)
                if p is None and j == STEPS - 1:
                    gate(0, None, 0)
                if valid(j + 3):
                    i = j + 3
                    n, t = at(p, i), i % T
                    if t == 0:
                        lo_done(pe, WGRP + n + KT - 1)
                    pe.wait_ge(s_qn, n)
                    b = WQ_BUF[i // T % 2]
                    for k in range(KT):
                        done = three(bank[0][:], xnT_hi[:, k, tile(t)], xnT_lo[:, k, tile(t)],
                                     wbuf(b, 0)[:, k, :], wbuf(b, 1)[:, k, :], k == 0, k == KT - 1)
                    done.then_inc(s_a, 1)
                if valid(j + 2):
                    i = j + 2
                    n, t = at(p, i), i % T
                    g = i // T if p is None else 2 * p + i // T
                    pe.wait_ge(s_qt, n + 1)
                    pe.wait_ge(s_sm, n)
                    for h in range(REP):
                        done = pe.matmul(bank[2][:, tile(h)], headT[:, tile(h)],
                                         keyT[:, bass.ds(g * TOK + t * P, P)], start=True, stop=True)
                    done.then_inc(s_c, 1)
                if valid(j + 1):
                    n = at(p, j + 1)
                    pe.wait_ge(s_pn, n + 1)
                    pe.wait_ge(s_pt, n)
                    for h in range(REP):
                        done = pe.transpose(bank[3][:, tile(h)], prob[:, tile(h)], ident[:])
                    done.then_inc(s_d, 1)
                if valid(j):
                    n, t = at(p, j), j % T
                    if t == 0:
                        lo_done(pe, WGRP + n + 2 * KT - 1)
                    if j == 0 and p is not None:
                        pe.wait_ge(s_ve1, 2 * T)
                    pe.wait_ge(s_al, n + 1)
                    pe.wait_ge(s_add, T + n)
                    b = WO_BUF[j // T % 2]
                    for h in range(REP):
                        done = three(bank[7][:], aoT_hi[:, tile(h)], aoT_lo[:, tile(h)],
                                     wbuf(b, 0)[:, h, :], wbuf(b, 1)[:, h, :], h == 0, h == REP - 1)
                    done.then_inc(s_f, 1)
                if j == -1:
                    values(2 * T - 1)
                    pe.wait_ge(s_ve1, 2 * T - 1)
                if valid(j + 1):
                    n = at(p, j + 1)
                    pe.wait_ge(s_ptl, n + 1)
                    if j >= 0:
                        pe.wait_ge(s_al, n)
                    three(bank[6][:], vcur_hi[:], vcur_lo[:], probT_hi[:], probT_lo[:], True, True)\
                        .then_inc(s_e, 1)

            for j in range(-3, 0):
                step(j, None)
                if j < -1:
                    values(2 * T + j)
            with pe.Fori(0, STEPS // BODY - 1) as p:
                for j in range(BODY):
                    step(j, p)
            def unit(i, p):
                for h in range(2):
                    gate(i, p, h)
                    down(i - 1, p, h, (0, 1))
                    up(i, p, h)
                    down(i - 1, p, h, (2, 3))

            for j in range(STEPS - BODY, STEPS):
                step(j, None)
            for t in range(HALF, T - 2):
                ln_transpose(3, t)
            up(0, None, 0, range(KT - 1))
            for t in range(T - 2, T):
                ln_transpose(3, t)
            up(0, None, 0, (KT - 1,))
            gate(0, None, 1)
            up(0, None, 1)
            unit(1, None)
            with pe.Fori(0, UNITS // 2 - 2) as p:
                for u in range(2):
                    unit(u + 2, p)
            for i in range(UNITS - 2, UNITS):
                unit(i, None)
            pe.wait_ge(s_ud, UNITS)
            last = (UNITS - 1) % 2
            taken = {0: 0, 1: 0}
            for h in range(2):
                if h == 0:
                    pe.wait_ge(s_hl, 2 * UNITS - 1)
                else:
                    pe.wait_ge(s_hll, 1)
                for c in range(KT):
                    if h == 1:
                        taken[(0, c) in POOL_DOWN] += 1
                        if (0, c) in POOL_DOWN:
                            pe.wait_ge(s_dsc, taken[1])
                        else:
                            pe.wait_ge(s_acc, T * (UNITS - 1) + taken[0])
                    elif c < 2:
                        pe.wait_ge(s_acc, T * (UNITS - 1) - 1 + c)
                    else:
                        pe.wait_ge(s_hm, 2 * UNITS - 3 + c)
                    w = unit_w(last, 3)[:, tile(c)]
                    for part in range(2):
                        done = pe.matmul(bank[4 + c][:], w, unit_h(last, part)[:, h * D:(h + 1) * D],
                                         start=(part == 0), stop=(part == 1))
                    done.then_inc(s_dn, 1)
            for t in range(T):
                by_pool = sum(h <= t // HALF for h, _ in POOL_DOWN)
                pe.wait_ge(s_acc, T * (UNITS - 1) + HALF * (t // HALF + 1) - by_pool)
                pe.wait_ge(s_dga, by_pool)
                if t >= 4:
                    pe.wait_ge(s_add, DONE + t - 3)
                for c in range(KT):
                    done = pe.transpose(bank[t % 4][:, tile(c)], accT[:, c, tile(t)], ident[:])
                done.then_inc(s_ot, 1)


def _program(nc, shapes):
    args = {n: nc.dram_tensor(f"in_{n}_dram", s, d, kind="ExternalInput").ap() for n, s, d in shapes}
    args["out"] = nc.dram_tensor("out_0_dram", (T, P, D), F32, kind="ExternalOutput").ap()
    cross_attention_ffn(nc, **args)


def kernel(**inputs):
    import numpy as np
    import concourse.bacc as bacc
    from concourse.bass_utils import run_bass_kernel_spmd

    a = {k: np.asarray(v) for k, v in inputs.items()}

    def rows(w):
        return w.T

    def blocks(w, n):
        return w.reshape(-1, P, w.shape[1] // n, n).transpose(2, 0, 1, 3)

    def units(w):
        return w.reshape(KT, P, UNITS, P).transpose(2, 1, 0, 3).reshape(UNITS, P, D)

    def unit_rows(w):
        return w.reshape(KT, UNITS, P).transpose(1, 0, 2).reshape(UNITS, D)

    laid = {
        "x": a["x"],
        "ctx": a["ctx_4096"],
        "ctxT": a["ctx_4096"].reshape(TOK, D).T.reshape(KT, P, TOK),
        "wk0": rows(a["L0_xattn_Wk"]).reshape(KT, P, D),
        "wq0": rows(a["L0_xattn_Wq"]).reshape(KT, P, D),
        "bqk": np.concatenate([a["L0_xattn_bq"].reshape(KT, P).T, a["L0_xattn_bk"].reshape(KT, P).T], 1),
        "wkey": blocks(rows(a["L1_xattn_k_proj_w"]), D).reshape(2 * KT, P, D),
        "wffn": rows(a["L0_ffn_W"]).reshape(KT, P, D),
        "wval": blocks(rows(a["L1_xattn_v_proj_w"]), D).reshape(2 * KT, P, D),
        "agT": rows(np.concatenate([a["L0_ffn_A"], a["L0_ffn_gate_w"]], 0))
            .reshape(KT, P, RMAX + NR).transpose(1, 0, 2),
        "bTb": np.concatenate([rows(a["L0_ffn_B"]), a["L0_ffn_b"][None]], 0),
        "gate_b": a["L0_ffn_gate_b"][None],
        "norm_w": np.stack([a["L1_xattn_q_norm_w"], a["L1_xattn_k_norm_w"]], 1),
        "mask": a["mask_1x1xSxS2_ff0"][0, 0],
        "wqo": np.concatenate([blocks(rows(a["L1_xattn_q_proj_w"]), D),
                               rows(a["L1_xattn_o_proj_w"]).reshape(NKV, REP, P, D)], 1).reshape(-1, P, D),
        "ffn_w": np.concatenate([units(a["L1_ffn_gate_w"]), units(a["L1_ffn_up_w"]),
                                 a["L1_ffn_down_w"].reshape(UNITS, P, D)], 2),
        "ffn_z": np.concatenate([unit_rows(a["L1_ffn_gate_z"]), unit_rows(a["L1_ffn_up_z"]),
                                 a["L1_ffn_down_z"]], 1),
        "up_s": unit_rows(a["L1_ffn_up_s"]),
        "gd_s": np.concatenate([a["L1_ffn_gate_s"].reshape(KT, UNITS, P).transpose(2, 1, 0),
                                a["L1_ffn_down_s"].reshape(UNITS, KT, P).transpose(2, 0, 1)], 2),
    }
    laid = {k: np.ascontiguousarray(v) for k, v in laid.items()}
    nc = bacc.Bacc("TRN2", target_bir_lowering=False, num_devices=1)
    _program(nc, [(k, v.shape, mybir.dt.from_np(v.dtype)) for k, v in laid.items()])
    r = run_bass_kernel_spmd(nc, [{f"in_{k}_dram": v for k, v in laid.items()}], core_ids=[0])
    return r.results[0]["out_0_dram"]
```
